# Optimizing a Trainium2 kernel written in Bass

```python
import numpy as np
import jax
import jax.numpy as jnp

def _softmax(x, axis=-1):
    return jax.nn.softmax(x, axis=axis)

def _gelu(x):
    return jax.nn.gelu(x, approximate=True)

def _silu(x):
    return jax.nn.silu(x)

def _sigmoid(x):
    return jax.nn.sigmoid(x)

def _layernorm(x, axis=-1, eps=1e-05):
    m = jnp.mean(x, axis=axis, keepdims=True)
    v = jnp.var(x, axis=axis, keepdims=True)
    return (x - m) / jnp.sqrt(v + eps)

def _scatter_add(tgt, idx, src, axis=0):
    return tgt.at[idx].add(src)

def _segment_sum(src, seg, n):
    return jax.ops.segment_sum(src, seg, n)
kernel_name = 'mk_flamingo_gated_d1_seqx_r4_a659da'

def setup_inputs(seed: int=0):
    np.random.seed(seed)
    _w = jnp.asarray

    def _rec_inputs():
        import jax
        import jax.numpy as jnp
        _rk = jax.random.key(seed)
        x = -0.0002928 + 1 * jax.random.normal(jax.random.fold_in(_rk, 1), (4, 512, 256), jnp.float32)
        _lenS = 512 - jax.random.randint(jax.random.fold_in(_rk, 7), (4,), 0, max(1, 512 // 4) + 1, jnp.int32)
        _lenS2 = 1024 - jax.random.randint(jax.random.fold_in(_rk, 8), (4,), 0, max(1, 1024 // 4) + 1, jnp.int32)
        _ctx_1024P = jax.random.normal(jax.random.fold_in(_rk, 11), (4, 16, 256), jnp.float32)
        _ctx_1024c = jax.random.dirichlet(jax.random.fold_in(_rk, 511), 0.3 * jnp.ones((16,), jnp.float32), (4, 1024))
        _ctx_1024t = jnp.einsum('bsk,bkd->bsd', _ctx_1024c, _ctx_1024P)
        _ctx_1024t = _ctx_1024t * jax.lax.rsqrt(jnp.mean(jnp.square(_ctx_1024t)) + 1e-12) * 0.953939
        ctx_1024 = -1.39393e-06 + 0.999914 * (_ctx_1024t + 0.3 * jax.random.normal(jax.random.fold_in(_rk, 611), (4, 1024, 256), jnp.float32))
        _validS = jnp.arange(512)[None, :] < _lenS[:, None]
        _validS2 = jnp.arange(1024)[None, :] < _lenS2[:, None]
        _causal = jnp.tril(jnp.ones((512, 512), dtype=bool))
        mask_BxS2_bf0 = jnp.logical_not(jnp.ones((4, 1024), dtype=bool))
        _g = jax.random.normal(jax.random.fold_in(_rk, 9001), (2, 1), jnp.float32)
        _g = jnp.sign(_g) * jnp.maximum(jnp.abs(_g), 1.0) + (_g == 0) * 1.0
        g_xattn = _g[0]
        g_ffn = _g[1]
        return (x, ctx_1024, mask_BxS2_bf0, g_xattn, g_ffn)
    x, ctx_1024, mask_BxS2_bf0, g_xattn, g_ffn = _rec_inputs()

    def _L0_xattn_setup():
        import jax, jax.numpy as jnp
        import numpy as np
        EMBED_DIM = 256
        NUM_HEADS = 16
        HEAD_DIM = EMBED_DIM // NUM_HEADS
        B, T, S = (2, 512, 512)
        key = jax.random.key(seed)
        ks = jax.random.split(key, 12)
        xavier = lambda k: jax.random.uniform(k, (EMBED_DIM, EMBED_DIM), jnp.float32, -np.sqrt(6.0 / (2 * EMBED_DIM)), np.sqrt(6.0 / (2 * EMBED_DIM)))
        return {'query': jax.random.normal(ks[0], (B, T, EMBED_DIM), jnp.float32), 'key': jax.random.normal(ks[1], (B, S, EMBED_DIM), jnp.float32), 'value': jax.random.normal(ks[2], (B, S, EMBED_DIM), jnp.float32), 'key_padding_mask': jnp.zeros((B, S), dtype=bool), 'Wq': xavier(ks[3]), 'bq': jnp.zeros((EMBED_DIM,), jnp.float32), 'Wk': xavier(ks[4]), 'bk': jnp.zeros((EMBED_DIM,), jnp.float32), 'Wv': xavier(ks[5]), 'bv': jnp.zeros((EMBED_DIM,), jnp.float32), 'Wo': xavier(ks[6]), 'bo': jnp.zeros((EMBED_DIM,), jnp.float32)}
    _L0_xattn_all = _L0_xattn_setup()
    _L0_xattn_in = {k: v for k, v in _L0_xattn_all.items() if k in ('Wq', 'bq', 'Wk', 'bk', 'Wv', 'bv', 'Wo', 'bo')}
    del _L0_xattn_all

    def _L0_ffn_setup():
        import jax, jax.numpy as jnp
        import numpy as np
        D_MODEL = 256
        EXPANSION = 4
        D_HIDDEN = D_MODEL * EXPANSION
        NUM_STAGES = int(np.log2(D_HIDDEN))

        def butterfly(y, weights, dim):
            lead = y.shape[:-1]
            for stage in range(weights.shape[0]):
                s = 2 ** stage
                nb = dim // (2 * s)
                yr = y.reshape(*lead, nb, 2, s)
                a = yr[..., 0, :]
                b = yr[..., 1, :]
                w = weights[stage].reshape(nb, s, 2, 2)
                na = w[..., 0, 0] * a + w[..., 0, 1] * b
                nb2 = w[..., 1, 0] * a + w[..., 1, 1] * b
                y = jnp.stack([na, nb2], axis=-2).reshape(*lead, dim)
            return y
        key = jax.random.key(seed)
        ks = jax.random.split(key, 6)
        B, S = (4, 512)
        x = jax.random.normal(ks[0], (B, S, D_MODEL), jnp.float32)
        W_exp = jax.random.normal(ks[1], (D_MODEL, D_HIDDEN), jnp.float32) * 0.02
        b_exp = jnp.zeros((D_HIDDEN,), jnp.float32)
        up_weights = jax.random.normal(ks[2], (NUM_STAGES, D_HIDDEN // 2, 2, 2), jnp.float32) * 0.02
        up_bias = jnp.zeros((D_HIDDEN,), jnp.float32)
        down_weights = jax.random.normal(ks[3], (NUM_STAGES, D_HIDDEN // 2, 2, 2), jnp.float32) * 0.02
        W_con = jax.random.normal(ks[4], (D_HIDDEN, D_MODEL), jnp.float32) * 0.02
        b_con = jnp.zeros((D_MODEL,), jnp.float32)
        down_bias = jnp.zeros((D_MODEL,), jnp.float32)
        return dict(x=x, W_exp=W_exp, b_exp=b_exp, up_weights=up_weights, up_bias=up_bias, down_weights=down_weights, W_con=W_con, b_con=b_con, down_bias=down_bias)
    _L0_ffn_all = _L0_ffn_setup()
    _L0_ffn_in = {k: v for k, v in _L0_ffn_all.items() if k in ('W_exp', 'b_exp', 'up_weights', 'up_bias', 'down_weights', 'W_con', 'b_con', 'down_bias')}
    del _L0_ffn_all
    return {'x': x, 'ctx_1024': ctx_1024, 'mask_BxS2_bf0': mask_BxS2_bf0, 'g_xattn': g_xattn, 'g_ffn': g_ffn, 'L0_xattn_Wq': _L0_xattn_in['Wq'], 'L0_xattn_bq': _L0_xattn_in['bq'], 'L0_xattn_Wk': _L0_xattn_in['Wk'], 'L0_xattn_bk': _L0_xattn_in['bk'], 'L0_xattn_Wv': _L0_xattn_in['Wv'], 'L0_xattn_bv': _L0_xattn_in['bv'], 'L0_xattn_Wo': _L0_xattn_in['Wo'], 'L0_xattn_bo': _L0_xattn_in['bo'], 'L0_ffn_W_exp': _L0_ffn_in['W_exp'], 'L0_ffn_b_exp': _L0_ffn_in['b_exp'], 'L0_ffn_up_weights': _L0_ffn_in['up_weights'], 'L0_ffn_up_bias': _L0_ffn_in['up_bias'], 'L0_ffn_down_weights': _L0_ffn_in['down_weights'], 'L0_ffn_W_con': _L0_ffn_in['W_con'], 'L0_ffn_b_con': _L0_ffn_in['b_con'], 'L0_ffn_down_bias': _L0_ffn_in['down_bias']}

def reference(x, ctx_1024, mask_BxS2_bf0, g_xattn, g_ffn, L0_xattn_Wq, L0_xattn_bq, L0_xattn_Wk, L0_xattn_bk, L0_xattn_Wv, L0_xattn_bv, L0_xattn_Wo, L0_xattn_bo, L0_ffn_W_exp, L0_ffn_b_exp, L0_ffn_up_weights, L0_ffn_up_bias, L0_ffn_down_weights, L0_ffn_W_con, L0_ffn_b_con, L0_ffn_down_bias):
    import jax
    import jax.numpy as jnp

    def _L0_xattn_ref(query, key, value, key_padding_mask, Wq, bq, Wk, bk, Wv, bv, Wo, bo):
        import jax, jax.numpy as jnp
        import numpy as np
        EMBED_DIM = 256
        NUM_HEADS = 16
        HEAD_DIM = EMBED_DIM // NUM_HEADS
        B, T, S = (2, 512, 512)
        bsz, tgt_len, _ = query.shape
        src_len = key.shape[1]
        q = (query @ Wq.T + bq).reshape(bsz, tgt_len, NUM_HEADS, HEAD_DIM).transpose(0, 2, 1, 3)
        k = (key @ Wk.T + bk).reshape(bsz, src_len, NUM_HEADS, HEAD_DIM).transpose(0, 2, 1, 3)
        v = (value @ Wv.T + bv).reshape(bsz, src_len, NUM_HEADS, HEAD_DIM).transpose(0, 2, 1, 3)
        scale = HEAD_DIM ** (-0.5)
        scores = jnp.einsum('bhtd,bhsd->bhts', q, k) * scale
        causal_mask = jnp.triu(jnp.ones((tgt_len, src_len), dtype=bool), k=1)
        neg_inf = jnp.finfo(scores.dtype).min
        scores = jnp.where(causal_mask[None, None], neg_inf, scores)
        scores = jnp.where(key_padding_mask[:, None, None, :], neg_inf, scores)
        attn = jax.nn.softmax(scores, axis=-1)
        out = jnp.einsum('bhts,bhsd->bhtd', attn, v)
        out = out.transpose(0, 2, 1, 3).reshape(bsz, tgt_len, EMBED_DIM)
        return out @ Wo.T + bo

    def _L0_ffn_ref(x, W_exp, b_exp, up_weights, up_bias, down_weights, W_con, b_con, down_bias):
        import jax, jax.numpy as jnp
        import numpy as np
        D_MODEL = 256
        EXPANSION = 4
        D_HIDDEN = D_MODEL * EXPANSION
        NUM_STAGES = int(np.log2(D_HIDDEN))

        def butterfly(y, weights, dim):
            lead = y.shape[:-1]
            for stage in range(weights.shape[0]):
                s = 2 ** stage
                nb = dim // (2 * s)
                yr = y.reshape(*lead, nb, 2, s)
                a = yr[..., 0, :]
                b = yr[..., 1, :]
                w = weights[stage].reshape(nb, s, 2, 2)
                na = w[..., 0, 0] * a + w[..., 0, 1] * b
                nb2 = w[..., 1, 0] * a + w[..., 1, 1] * b
                y = jnp.stack([na, nb2], axis=-2).reshape(*lead, dim)
            return y
        h = jnp.einsum('bsd,dh->bsh', x, W_exp) + b_exp
        h = butterfly(h, up_weights, D_HIDDEN)
        h = jax.nn.gelu(h + up_bias, approximate=False)
        h = butterfly(h, down_weights, D_HIDDEN)
        y = jnp.einsum('bsh,hd->bsd', h, W_con) + b_con
        return y + down_bias
    x = x + jnp.tanh(g_xattn[0]) * _L0_xattn_ref(_layernorm(x, axis=-1), ctx_1024, ctx_1024, mask_BxS2_bf0, L0_xattn_Wq, L0_xattn_bq, L0_xattn_Wk, L0_xattn_bk, L0_xattn_Wv, L0_xattn_bv, L0_xattn_Wo, L0_xattn_bo)
    x = x + jnp.tanh(g_ffn[0]) * _L0_ffn_ref(_layernorm(x, axis=-1), L0_ffn_W_exp, L0_ffn_b_exp, L0_ffn_up_weights, L0_ffn_up_bias, L0_ffn_down_weights, L0_ffn_W_con, L0_ffn_b_con, L0_ffn_down_bias)
    return x

_drawn_inputs = setup_inputs


def setup_inputs(seed=0):
    import zlib

    import numpy as np

    out = dict(_drawn_inputs(seed))
    spreads = {'L0_xattn_bq': (0.0, 0.438),
     'L0_xattn_bk': (0.0, 0.8),
     'L0_xattn_bv': (0.0, 0.1),
     'L0_xattn_bo': (0.0, 0.1),
     'L0_ffn_b_exp': (0.0, 0.1),
     'L0_ffn_up_bias': (0.0, 0.1),
     'L0_ffn_b_con': (0.0, 0.1),
     'L0_ffn_down_bias': (0.0, 0.1)}
    factors = {}
    for name, (base, spread) in spreads.items():
        noise = np.random.default_rng([zlib.crc32(name.encode()), seed]).standard_normal(out[name].shape)
        drawn = base * np.exp(spread * noise) if base else spread * noise
        out[name] = jnp.asarray(drawn.astype(out[name].dtype))
    for name, factor in factors.items():
        out[name] = (out[name] * factor).astype(out[name].dtype)
    return out
```

```python
from contextlib import ExitStack

import concourse.bass as bass
from concourse import mybir

P = 128
F32 = mybir.dt.float32
BF16 = mybir.dt.bfloat16
U8 = mybir.dt.uint8
ALU = mybir.AluOpType
ACT = mybir.ActivationFunctionType
AX_X = mybir.AxisListType.X

NEG = -1.0e30
FLOOR = -1.0e25
EPS = 1.0e-5
MISC = 2
ST_RING = 3
SM_RING = 2
P_RING = 8
TERMS = ((0, 0), (0, 1), (1, 0), (1, 1), (0, 2), (2, 0))


def plan(NB, HG, NT, NI, LOW, pieces):
    order = []

    def front(b):
        return ([("XT", b, 0), ("CT", b, 0)] + [(w, b, m) for m in range(2) for w in ("QP", "KP")]
                + [("VP", b, u) for u in range(2)] + [("STK", b, 0)])

    order += [("LN1", 0, 0), ("WT", 0, 0), ("PAD", 0, 0)] + front(0) + [("FT", 0, 0)]
    prep = [("EW", 0, u) for u in range(4)]
    prep += [("SEL", k, u) for k in range(LOW) for u in range(1 if k < 5 else 2 if k == 5 else 4)]
    prep += [("DTR", 0, u) for u in range(2)] + [("UB", 0, t) for t in range(NI)] + [("UST", 0, 0)]
    prep += [("DST", 0, 0)] + [("DB", 0, u) for u in range(4)] + [("UT", 0, u) for u in range(4)]
    prep += [("CM", 0, 0), ("VM", 0, 0)] + [("MP", b, 0) for b in range(NB)] + [("BASE", 0, 0)]
    prep = merge(prep, [("CS", 0, n) for n in range(pieces)])
    k = prep.index(("CM", 0, 0))
    prep = [s for s in prep[:k] + [("CS", 0, n) for n in range(pieces) if ("CS", 0, n) in prep[k:]]
            + [s for s in prep[k:] if s[0] != "CS"]]
    units = [("SM", 0, u) for u in range(10 * HG)]
    order += merge(units, prep) + [("MR", 0, 0)]
    for b in range(NB + 1):
        fill = []
        if b >= 1:
            fill += [("OT", b - 1, 0)] + [("OP", b - 1, i) for i in range(NT)] + [("YT", b - 1, 0)]
        if b >= 1:
            fill += [("F1", b - 1, i) for i in range(NI)]
        if b + 1 < NB:
            fill += front(b + 1) + [("BASE", b + 1, 0)]
        if b >= 1:
            fill += [("F2", b - 1, i) for i in range(NT)]
        if b + 1 < NB:
            fill += [("SM", b + 1, u) for u in range(10 * HG)] + [("MR", b + 1, 0)]
        if b < NB:
            order += merge(attention(b, HG), fill)
        else:
            order += fill
    turn, n = {}, 0
    for name, b, i in order:
        for j in range({"WT": 4, "XT": 2, "YT": 2, "CT": 2, "OT": 2, "UB": 1}.get(name, 1)
                       if name in USES else 0):
            turn[(name, b, i, j)] = n
            n += 1
    return order, turn


USES = ("WT", "XT", "YT", "CT", "OT", "QP", "KP", "VP", "FT", "EW", "SEL", "DTR", "UB", "DB", "UT",
        "CM", "VM", "MP", "MR", "NM", "OP", "F1", "F2")


def attention(b, HG):
    out = []
    for g in range(HG):
        for r in range(10):
            out.append(("ST", b, 10 * g + r))
            if r == 1 and g:
                out += [("PV", b, 3 * g - 1), ("NM", b, g - 1)]
            if r in (5, 9):
                out.append(("PV", b, 3 * g + (r == 9)))
    return out + [("PV", b, 3 * HG - 1), ("NM", b, HG - 1)]


def merge(main, fill):
    out, j = [], 0
    for n, x in enumerate(main):
        out.append(x)
        upto = (n + 1) * len(fill) // len(main)
        out += fill[j:upto]
        j = upto
    return out


def flamingo_block(nc, x, ctx_in, mask, g_xattn, g_ffn, Wq, bq, Wk, bk, Wv, bv, Wo, bo,
                   W_exp, b_exp, up_w, up_b, dn_w, W_con, b_con, dn_b, ident_in, iota_in,
                   select_in, out):
    NB, T, D = x.shape
    S = ctx_in.shape[1]
    H, HD = 16, D // 16
    NT = T // P
    KC = D // P
    NH = W_exp.shape[1]
    NI = NH // P
    STAGES = up_w.shape[0]
    LOW = 7
    HG = H // 4
    KROWS = 16 * len(TERMS)
    SCALE = float(HD) ** -0.5
    assert (T, D, NH, STAGES, HD) == (512, 256, 1024, 10, 16)

    order, turn = plan(NB, HG, NT, NI, LOW, NB * S // 256)

    with ExitStack() as ctx:
        def sb(name, shape, dt=F32):
            return ctx.enter_context(nc.sbuf_tensor(name, shape, dt))

        def ps(name, shape=(P, 512), dt=F32):
            return ctx.enter_context(nc.psum_tensor(name, list(shape), dt))

        def sem(name):
            return ctx.enter_context(nc.semaphore(name))

        ST = [ps(f"ps_st{i}") for i in range(ST_RING)]
        SM = [ps(f"ps_sm{i}") for i in range(SM_RING)]
        OACC = ps("ps_oacc")
        MB = [ps(f"ps_misc{i}") for i in range(MISC)]

        ident = sb("ident", [P, P])
        tri = sb("tri", [P, T], BF16)
        stack0 = sb("stack0", [P, 2 * 4096])
        stack1 = sb("stack1", [P, 2 * 4096])
        X = sb("X", [P, NB * NT, D])
        xn = sb("xn", [P, NT, D])
        xnT = sb("xnT", [P, KC, T])
        ctxA = sb("ctxA", [P, NT, D])
        ctxT = sb("ctxT", [P, KC, T])
        qf, kf = sb("qf", [P, T]), sb("kf", [P, T])
        qp, kp = sb("qp", [P, 3, T], BF16), sb("kp", [P, 3, T], BF16)
        Vs = [sb(f"Vs{i}", [P, NT, H, 32]) for i in range(2)]
        probs = sb("probs", [P, P_RING * T + 64])
        oT = sb("oT", [P, 2, T])
        On = sb("On", [P, 2 * 1024 + 8])
        Wu = sb("Wu", [P, KC, NH])
        Wd = sb("Wd", [P, NI, D])
        hT = sb("hT", [P, NI, T])
        WT = sb("WT", [P, 4, KC, D])
        rows = sb("rows", [P, 3, D])
        mp = sb("mp", [P, NB, D])
        ob = sb("ob", [P, 2, D])
        cols = sb("cols", [P, 64])
        small = sb("small", [P, 512 // 4])
        rowmax = sb("rowmax", [P, H, NT])
        mparts = sb("mparts", [4 * H, 3, P], BF16)
        pool_tmp = sb("pool_tmp", [P, 2, D])
        mrest = sb("mrest", [4 * H, P])
        tg = sb("tg", [P, 4])
        mean32 = sb("mean32", [P, 32])
        stage79 = sb("stage79", [P, 2, 3, 4, 4])
        lnst = sb("lnst", [P, NT, 6])
        mv1 = sb("mv1", [P, NB * NT, 2])
        r1 = sb("r1", [P, 4, NB * NT])
        mv2 = sb("mv2", [P, NT, 2])
        r2 = sb("r2", [P, 4, NT])
        padb = sb("padb", [NB, T], BF16)

        bq_c, bk_c, bv_c = cols[:, 0:2], cols[:, 2:4], cols[:, 4:6]
        upb_c, bexp_c, hb = cols[:, 8:16], cols[:, 16:24], cols[:, 24:32]
        fcol = cols[:, 32:48].rearrange("p (t b) -> p t b", b=NB)
        cmT = small[:, 0:8].rearrange("p (c b) -> p c b", b=NB)
        mvT = small[:, 8:16].rearrange("p (c b) -> p c b", b=NB)
        negmax = small[:, 32:96]
        den = small[:, 96:112]
        rden = small[:, 112:128]

        def stacks(buf):
            v = buf[:, :].bitcast(BF16).rearrange("p (w h t) -> p w h t", w=2, t=T)
            return v[:, 0], v[:, 1]

        Qs, Ks = zip(*(stacks(s) for s in (stack0, stack1)))

        wexp = stack1[:, 0:2048].rearrange("p (c n) -> p c n", c=KC)
        wcon = stack1[:, 2048:4096].rearrange("p (t d) -> p t d", d=D)
        chain_odd = stack1[:, 4096:6144].rearrange("p (w n) -> p w n", w=2)
        chain_even = stack1[:, 6144:7168].rearrange("p (w n) -> p w n", w=2)
        dnT = stack1[:, 7168:8192].rearrange("p (t j) -> p t j", j=P)
        wexpT = On[:, 0:NI * (D + 1)].rearrange("p (t c) -> p t c", c=D + 1)
        upY = probs[:, 0:NI * (D + 1)].rearrange("p (t c) -> p t c", c=D + 1)
        sel6 = probs[0:1, 2056:4104].rearrange("p (t n) -> p t n", t=NI)
        wlow = hT[:, :, :].rearrange("p t n -> p (t n)")
        esel = Vs[1][0:64].rearrange("p t h c -> p (t h c)")[:, 0:2 * LOW * P].rearrange(
            "p (s m) -> p s m", m=P)
        wraw = On[:, 0:2048].rearrange("p (w m c) -> p w m c", w=4, c=D)
        cpart = oT[:, :, :]
        csum = hT[:, NI - 1, :]
        mp_flat = mp[:, :, :].rearrange("p b d -> p (b d)")
        up_tmp = [mp_flat[:, 256:256 + D + 1], mp_flat[:, 520:520 + D + 1]]
        down_tmp = [ob[:, 1, :], mp[:, 0, :]]
        scratch = nc.dram_tensor("qk_parts", (NB, 2, 3, D, T), BF16, kind="Internal").ap()
        pad_u8 = xnT[0:NB, 1, 0:T // 4].bitcast(U8)
        padf = xn[0:NB, 0:2, :].rearrange("p a b -> p (a b)")
        iota = xn[0:NB, 2:4, :].rearrange("p a b -> p (a b)")
        padt = xnT[0:NB, 0, :]
        first_key = cols[0:NB, 48:49]
        allpad = ob[0:NB, :, :].rearrange("p a b -> p (a b)")

        On_v = On[:, 0:1024].rearrange("p (t n) -> p t n", n=D)
        OnT = On[:, 1024:2048].rearrange("p (c n) -> p c n", c=KC)

        def wlow_of(k):
            n = 64 << k
            off = 64 * ((1 << k) - 1)
            return wlow[0:64 >> k, off:off + n].rearrange("p (w t n) -> p w t n", w=2, t=NI)

        loaded = {n: sem("ld_" + n) for n in
                  ("ident", "w", "rows", "cols", "mask", "select", "wexp", "wcon", "wlow",
                   "sel6a", "sel6b", "stage79", "gate")}
        x_loaded = [sem(f"x_loaded{b}") for b in range(NB)]
        ctx_loaded = [sem(f"ctx_loaded{b}") for b in range(NB)]
        cpart_loaded = [sem(f"cpart_loaded{i}") for i in range(2)]
        q_written = [sem(f"q_written{b}") for b in range(NB)]
        k_written = [sem(f"k_written{b}") for b in range(NB)]
        stack_loaded = [sem(f"stack_loaded{b}") for b in range(NB)]
        maxrow_loaded = [sem(f"maxrow_loaded{b}") for b in range(NB)]
        stored = [sem(f"stored{i}") for i in range(2)]
        filled = [sem(f"misc_filled{i}") for i in range(MISC)]
        drained = [sem(f"misc_drained{i}") for i in range(MISC)]
        st_filled, exp_done, mask_done = sem("st_filled"), sem("exp_done"), sem("mask_done")
        pv_done, oacc_drained = sem("pv_done"), sem("oacc_drained")
        sm_filled, max_done = sem("sm_filled"), sem("max_done")
        q_split, k_split = sem("q_split"), sem("k_split")
        xn_ready, var_ready, std_ready = sem("xn_ready"), sem("var_ready"), sem("std_ready")
        base_ready, y_based, up_staged = sem("base_ready"), sem("y_based"), sem("up_staged")
        cpart_used, pad_ready, const_ready = sem("cpart_used"), sem("pad_ready"), sem("const_ready")
        negmax_ready, mparts_ready = sem("negmax_ready"), sem("mparts_ready")
        tanh_ready, csum_ready, down_staged = sem("tanh_ready"), sem("csum_ready"), sem("down_staged")
        stack1_const, wexpT_ready = sem("stack1_const"), sem("wexpT_ready")
        tri_ready = sem("tri_ready")
        dve_step, pool_step = sem("dve_step"), sem("pool_step")

        def bank(*key):
            return MB[turn[key] % MISC]

        def wait_filled(eng, *key):
            eng.wait_ge(filled[turn[key] % MISC], turn[key] // MISC + 1)

        def wait_drained(eng, *key):
            eng.wait_ge(drained[turn[key] % MISC], turn[key] // MISC + 1)

        def drain(ins, *key):
            ins.then_inc(drained[turn[key] % MISC], 1)

        xn_turn = {s[:2]: n for n, s in enumerate(s for s in order if s[0] in ("XT", "YT"))}
        xn_keys = [s for s in order if s[0] in ("XT", "YT")]

        def last_reader_of_xnT(k):
            name, b, _ = xn_keys[k]
            return ("QP", b, 1, 0) if name == "XT" else ("F1", b, NI - 1, 0)

        def burst_of(n):
            return 3 * (n // 10) + (0 if n % 10 < 4 else 1 if n % 10 < 8 else 2)

        block = ctx.enter_context(nc.Block())

        @block.sync
        def _(sp):
            def load(name, dst, src):
                sp.dma_start(dst, src).then_inc(loaded[name], 16)

            load("ident", ident[:, :], ident_in)
            for b in range(NB):
                sp.dma_start(X[:, NT * b:NT * b + NT, :],
                             x[b].rearrange("(i p) d -> p i d", p=P)).then_inc(x_loaded[b], 16)
                if b == 0:
                    for i, w in enumerate((Wq, Wk, Wv, Wo)):
                        load("w", wraw[:, i], w.rearrange("(m p) c -> p m c", p=P))
                    load("mask", pad_u8, mask[:, 0:T])
                    load("mask", iota, iota_in)
                    sp.dma_start(ctxA[:, :, :], ctx_in[0, 0:T].rearrange("(i p) d -> p i d", p=P)
                                 ).then_inc(ctx_loaded[0], 16)
                    for src, dst in ((bq, bq_c), (bk, bk_c), (bv, bv_c), (up_b, upb_c),
                                     (b_exp, bexp_c)):
                        sp.dma_start(dst, src.rearrange("(c p) -> p c", p=P),
                                     allow_slow_non_contiguous=True).then_inc(loaded["cols"], 16)
            for i, r in enumerate((bv, bo, b_con)):
                load("rows", rows[:, i, :], r.partition_broadcast(P))
            load("rows", ob[:, 0, :], dn_b.partition_broadcast(P))
            load("gate", tg[:, 0:1], g_xattn.partition_broadcast(P))
            load("gate", tg[:, 1:2], g_ffn.partition_broadcast(P))
            load("wexp", wexp, W_exp.rearrange("(c p) n -> p c n", p=P))
            load("select", esel, select_in)
            for k in range(LOW - 1):
                for w, src in enumerate((up_w, dn_w)):
                    load("wlow", wlow_of(k)[:, w],
                         src[k].rearrange("(t q u) a c -> q t (u a c)", t=NI, u=1 << k))
            load("sel6a", sel6, up_w[6].rearrange("(o t u) a c -> o t (u a c)", o=1, t=NI))
            load("wcon", wcon, W_con.rearrange("(t p) d -> p t d", p=P))
            for w, src in enumerate((up_w, dn_w)):
                for e in range(STAGES - LOW):
                    load("stage79", stage79[:, w, e],
                         src[LOW + e].rearrange("(g p) a c -> p g (a c)", p=P))

            stores = 0
            for name, b, i in order:
                if name in ("QP", "KP"):
                    parts, split, done, w = ((qp, q_split, q_written, 0) if name == "QP" else
                                             (kp, k_split, k_written, 1))
                    sp.wait_ge(split, 2 * b + i + 1)
                    sp.dma_start(scratch[b, w, :, P * i:P * i + P, :].rearrange("s p t -> p s t"),
                                 parts[:, :, :]).then_inc(done[b], 16)
                elif name == "VP" and i == 1 and b + 1 < NB:
                    wait_filled(sp, "CT", b, 0, 1)
                    sp.dma_start(ctxA[:, :, :], ctx_in[b + 1, 0:T].rearrange("(i p) d -> p i d", p=P)
                                 ).then_inc(ctx_loaded[b + 1], 16)
                elif name == "STK":
                    if b >= 2:
                        sp.wait_ge(st_filled, 10 * HG * (b - 1))
                    if b == 1:
                        sp.wait_ge(stack1_const, 1)
                    sp.wait_ge(q_written[b], 16 * KC)
                    sp.wait_ge(k_written[b], 16 * KC)
                    for r, pair in enumerate(TERMS):
                        for w, dst in enumerate((Qs[b % 2], Ks[b % 2])):
                            sp.dma_start(dst[HD * r:HD * r + HD, :, :],
                                         scratch[b, w, pair[w]].rearrange("(h d) t -> d h t", d=HD)
                                         ).then_inc(stack_loaded[b], 16)
                    sp.wait_ge(pad_ready, 1)
                    sp.wait_ge(stack1_const if b % 2 else const_ready, 1)
                    sp.dma_start(Ks[b % 2][KROWS:KROWS + 1, :, :],
                                 padb[b:b + 1, :].unsqueeze(1).to_broadcast([1, H, T])
                                 ).then_inc(stack_loaded[b], 16)
                elif name == "MR":
                    sp.wait_ge(mparts_ready, b + 1)
                    if b == 0:
                        sp.wait_ge(const_ready, 1)
                    for s in range(3):
                        sp.dma_start(Qs[b % 2][KROWS + 1 + s:KROWS + 2 + s, :, :].rearrange(
                            "p h t -> p (h t)"), mparts[:, s, :]).then_inc(maxrow_loaded[b], 16)
                elif name == "CS":
                    if i >= 2:
                        sp.wait_ge(cpart_used, i - 1)
                    sp.dma_start(cpart[:, i % 2, :].rearrange("p (r d) -> p r d", r=2),
                                 ctx_in[i // 4, 256 * (i % 4):256 * (i % 4) + 256].rearrange(
                                     "(p r) d -> p r d", r=2)).then_inc(cpart_loaded[i % 2], 16)
                elif name == "SEL" and b == 6 and i == 1:
                    wait_filled(sp, "SEL", 6, 1, 0)
                    load("sel6b", sel6, dn_w[6].rearrange("(o t u) a c -> o t (u a c)", o=1, t=NI))
                elif name == "F2":
                    wait_drained(sp, "F2", b, i, 0)
                    sp.dma_start(out[b, P * i:P * i + P, :], ob[:, i % 2, :]).then_inc(
                        stored[i % 2], 16)
                    stores += 1
            for s in stored:
                sp.wait_ge(s, 16 * (stores // 2))

        @block.gpsimd
        def _(pool):
            steps = [0]

            def link(ins):
                steps[0] += 1
                ins.then_inc(pool_step, 1)
                pool.wait_ge(pool_step, steps[0])

            link(pool.memset(tri[:, :], 0.0))
            pool.affine_select(out=tri[:, T - P:T], in_=tri[:, T - P:T], compare_op=ALU.is_ge,
                               fill=NEG, base=0, pattern=[[-1, P]],
                               channel_multiplier=1).then_inc(tri_ready, 1)
            link(pool.memset(mean32[:, :], 1.0 / S))
            link(pool.memset(Qs[0][KROWS:KROWS + 4, :, :], 1.0))
            link(pool.memset(Vs[0][:, :, :, HD:32], 0.0))
            link(pool.memset(Vs[0][:, :, :, HD:HD + 1], 1.0))
            pool.memset(Ks[0][KROWS:KROWS + 4, :, :], 1.0).then_inc(const_ready, 1)
            pool.wait_ge(const_ready, 1)

            for name, b, i in order:
                if name == "KP":
                    wait_drained(pool, "KP", b, i, 0)
                    link(pool.tensor_tensor(kf[:, :], kf[:, :], kp[:, 0, :], ALU.subtract))
                    link(pool.tensor_copy(kp[:, 1, :], kf[:, :]))
                    pool.tensor_tensor(kp[:, 2, :], kf[:, :], kp[:, 1, :],
                                       ALU.subtract).then_inc(k_split, 1)
                elif name == "DST":
                    pool.wait_ge(loaded["wcon"], 16)
                    pool.wait_ge(loaded["stage79"], 16 * 2 * (STAGES - LOW))
                    wait_filled(pool, "FT", 0, 0, 0)
                    ta, tb = down_tmp
                    for e in reversed(range(STAGES - LOW)):
                        for a in range(NI):
                            if a & (1 << e):
                                continue
                            c = a + (1 << e)
                            g = (a >> (e + 1)) * (1 << e) + a % (1 << e)
                            w = stage79[:, 1, e, g, :]
                            pool.tensor_scalar(ta, wcon[:, a, :], w[:, 0:1], None, ALU.mult)
                            link(pool.tensor_scalar(tb, wcon[:, a, :], w[:, 1:2], None, ALU.mult))
                            link(pool.tensor_scalar(pool_tmp[:, 0, :], wcon[:, c, :], w[:, 2:3],
                                                    None, ALU.mult))
                            link(pool.tensor_scalar(wcon[:, c, :], wcon[:, c, :], w[:, 3:4],
                                                    None, ALU.mult))
                            pool.tensor_tensor(wcon[:, a, :], pool_tmp[:, 0, :], ta, ALU.add)
                            ins = pool.tensor_tensor(wcon[:, c, :], wcon[:, c, :], tb, ALU.add)
                            if e == 0 and c == NI - 1:
                                ins.then_inc(down_staged, 1)
                            else:
                                link(ins)
                elif name == "BASE":
                    pool.wait_ge(tanh_ready, 2)
                    pool.wait_ge(xn_ready, xn_turn[("XT", b)] + 1)
                    wait_drained(pool, "MP", b, 0, 0)
                    wait_drained(pool, "FT", 0, 0, 0)
                    for t in range(NT):
                        xt = X[:, NT * b + t, :]
                        pool.tensor_tensor(xt, xt, rows[:, 1, :], ALU.add)
                        tmp = pool_tmp[:, t % 2, :]
                        if NT * b + t >= 2:
                            pool.wait_ge(base_ready, NT * b + t - 1)
                        link(pool.tensor_scalar(tmp, mp[:, b, :], fcol[:, t, b:b + 1],
                                                None, ALU.mult))
                        pool.tensor_tensor(xt, xt, tmp,
                                           ALU.add).then_inc(base_ready, 1)
                elif name == "UT" and i == 3:
                    wait_filled(pool, "DB", 0, 3, 0)
                    wait_filled(pool, "UT", 0, 3, 0)
                    wait_filled(pool, "SEL", LOW - 1, 3, 0)
                    wait_drained(pool, "UT", 0, 3, 0)
                    link(pool.memset(Vs[1][:, :, :, HD:32], 0.0))
                    link(pool.memset(Vs[1][:, :, :, HD:HD + 1], 1.0))
                    link(pool.memset(Qs[1][KROWS:KROWS + 4, :, :], 1.0))
                    pool.memset(Ks[1][KROWS:KROWS + 4, :, :], 1.0).then_inc(stack1_const, 1)
                    pool.wait_ge(stack1_const, 1)
                elif name == "ST":
                    n = 10 * HG * b + i
                    pool.wait_ge(exp_done, n + 1)
                    p = probs[:, T * (n % P_RING):T * (n % P_RING) + T]
                    r = i % 10
                    step = T if r < 4 else 3 * P if r < 8 else 2 * P
                    v = (p[:, 0:P].unsqueeze(1) if r < 4 else
                         p.rearrange("p (n c) -> p n c", c=P)[:, 0::step // P, :])
                    nblk = 1 if r < 4 else 2
                    pool.affine_select(out=v, in_=v, compare_op=ALU.is_ge, fill=0.0, base=0,
                                       pattern=[[0, nblk], [1, P]],
                                       channel_multiplier=-1).then_inc(mask_done, 1)
                elif name == "YT":
                    pool.wait_ge(xn_ready, xn_turn[("YT", b)] + 1)
                    for t in range(NT):
                        xt = X[:, NT * b + t, :]
                        pool.tensor_tensor(xt, xt, rows[:, 2, :], ALU.add).then_inc(y_based, 1)

        @block.scalar
        def _(act):
            act.wait_ge(loaded["gate"], 32)
            act.activation(tg[:, 2:4], tg[:, 0:2], ACT.Tanh).then_inc(tanh_ready, 1)
            for name, b, i in order:
                if name == "LN1":
                    act.wait_ge(var_ready, 1)
                    act.activation(r1[:, 1, :], r1[:, 0, :], ACT.Sqrt).then_inc(std_ready, 1)
                elif name in ("XT", "YT", "CT", "OT"):
                    dst = {"CT": ctxT, "OT": OnT}.get(name, xnT)
                    if name == "YT":
                        act.wait_ge(var_ready, b + 2)
                        act.activation(r2[:, 1, :], r2[:, 0, :], ACT.Sqrt).then_inc(std_ready, 1)
                    if name in ("XT", "YT") and xn_turn[(name, b)] > 0:
                        wait_filled(act, *last_reader_of_xnT(xn_turn[(name, b)] - 1))
                    if name == "CT" and b > 0:
                        wait_filled(act, "KP", b - 1, 1, 0)
                        wait_filled(act, "VP", b - 1, 1, 0)
                    if name == "OT" and b > 0:
                        wait_filled(act, "OP", b - 1, NT - 1, 0)
                    for c in range(KC):
                        wait_filled(act, name, b, i, c)
                        drain(act.copy(dst[:, c, :], bank(name, b, i, c)[:, :]), name, b, i, c)
                elif name in ("QP", "KP"):
                    f, parts, bias, split, done = ((qf, qp, bq_c, q_split, q_written)
                                                   if name == "QP" else
                                                   (kf, kp, bk_c, k_split, k_written))
                    n = 2 * b + i
                    if n > 0:
                        act.wait_ge(split, n)
                        act.wait_ge(done[(n - 1) // 2], 16 * ((n - 1) % 2 + 1))
                    act.wait_ge(loaded["cols"], 80)
                    wait_filled(act, name, b, i, 0)
                    pq = bank(name, b, i, 0)
                    act.activation(f[:, :], pq[:, :], ACT.Identity, bias=bias[:, i:i + 1])
                    drain(act.activation(parts[:, 0, :], pq[:, :], ACT.Identity,
                                         bias=bias[:, i:i + 1]), name, b, i, 0)
                elif name == "MP":
                    wait_filled(act, "MP", b, 0, 0)
                    act.wait_ge(down_staged, 1)
                    act.wait_ge(up_staged, 1)
                    drain(act.copy(mp[:, b, :], bank("MP", b, 0, 0)[:, 0:D]), "MP", b, 0, 0)
                elif name == "ST":
                    n = 10 * HG * b + i
                    if n >= P_RING:
                        act.wait_ge(pv_done, burst_of(n - P_RING) + 1)
                    if n == 0:
                        wait_filled(act, "UT", 0, 3, 0)
                        wait_filled(act, "SEL", LOW - 1, 3, 0)
                    act.wait_ge(st_filled, n + 1)
                    act.activation(probs[:, T * (n % P_RING):T * (n % P_RING) + T],
                                   ST[n % ST_RING][:, :], ACT.Exp, scale=SCALE).then_inc(exp_done, 1)
                elif name == "NM":
                    G = HG * b + i
                    act.wait_ge(pv_done, 3 * (G + 1))
                    if G == 0:
                        act.wait_ge(cpart_used, NB * S // 256)
                    if G >= 2:
                        wait_filled(act, "NM", (G - 2) // HG, (G - 2) % HG, 0)
                    act.copy(oT[:, G % 2, :], OACC[:, :]).then_inc(oacc_drained, 1)
                elif name == "F1":
                    if b > 0:
                        wait_filled(act, "F2", b - 1, NT - 1, 0)
                    wait_filled(act, "F1", b, i, 0)
                    act.wait_ge(up_staged, 1)
                    drain(act.activation(hT[:, i, :], bank("F1", b, i, 0)[:, :], ACT.Gelu,
                                         bias=hb[:, i:i + 1]), "F1", b, i, 0)

        @block.vector
        def _(dve):
            steps = [0]

            def link(ins):
                steps[0] += 1
                ins.then_inc(dve_step, 1)
                dve.wait_ge(dve_step, steps[0])

            def inverse_std(r):
                link(dve.reciprocal(r[:, 2, :], r[:, 1, :]))
                link(dve.tensor_tensor(r[:, 3, :], r[:, 2, :], r[:, 2, :], ALU.mult))
                link(dve.tensor_tensor(r[:, 3, :], r[:, 3, :], r[:, 0, :], ALU.mult))
                link(dve.tensor_scalar(r[:, 3, :], r[:, 3, :], -0.5, 1.5, ALU.mult, ALU.add))
                link(dve.tensor_tensor(r[:, 2, :], r[:, 2, :], r[:, 3, :], ALU.mult))

            for name, b, i in order:
                if name == "LN1":
                    for t in range(NB * NT):
                        if t % NT == 0:
                            dve.wait_ge(x_loaded[t // NT], 16)
                        link(dve.bn_stats(lnst[:, t % NT, :], X[:, t, :]))
                        link(dve.bn_aggr(mv1[:, t, :], lnst[:, t % NT, :]))
                    dve.tensor_scalar(r1[:, 0, :], mv1[:, :, 1], EPS, None,
                                      ALU.add).then_inc(var_ready, 1)
                    dve.wait_ge(std_ready, 1)
                    inverse_std(r1)
                elif name == "WT":
                    for w in range(4):
                        wait_filled(dve, "WT", 0, 0, w)
                        if w == 3:
                            dve.wait_ge(tanh_ready, 1)
                        src = bank("WT", 0, 0, w)[:, :]
                        dst = WT[:, w].rearrange("p c n -> p (c n)")
                        drain(dve.tensor_copy(dst, src) if w < 3 else
                              dve.tensor_scalar(dst, src, tg[:, 2:3], None, ALU.mult),
                              "WT", 0, 0, w)
                    dve.wait_ge(loaded["rows"], 64)
                    link(dve.tensor_tensor(rows[:, 2, :], rows[:, 2, :], ob[:, 0, :], ALU.add))
                    link(dve.tensor_scalar(rows[:, 2, :], rows[:, 2, :], tg[:, 3:4], None, ALU.mult))
                    dve.tensor_scalar(rows[:, 1, :], rows[:, 1, :], tg[:, 2:3], None,
                                      ALU.mult).then_inc(tanh_ready, 1)
                elif name == "PAD":
                    dve.wait_ge(loaded["mask"], 32)
                    link(dve.tensor_copy(padf, pad_u8))
                    dve.tensor_scalar(padb[:, :], padf, NEG, None, ALU.mult).then_inc(pad_ready, 1)
                    link(dve.scalar_tensor_tensor(out=padt, in0=padf, scalar=1.0e6, in1=iota,
                                                  op0=ALU.mult, op1=ALU.add))
                    link(dve.tensor_reduce(first_key, padt, AX_X, ALU.min))
                    dve.tensor_scalar(allpad, iota, first_key, None,
                                      ALU.is_lt).then_inc(pad_ready, 1)
                elif name in ("XT", "YT"):
                    k = xn_turn[(name, b)]
                    if name == "YT":
                        for t in range(NT):
                            wait_drained(dve, "OP", b, t, 0)
                            link(dve.bn_stats(lnst[:, t, :], X[:, NT * b + t, :]))
                            link(dve.bn_aggr(mv2[:, t, :], lnst[:, t, :]))
                        dve.tensor_scalar(r2[:, 0, :], mv2[:, :, 1], EPS, None,
                                          ALU.add).then_inc(var_ready, 1)
                        dve.wait_ge(std_ready, b + 2)
                        inverse_std(r2)
                    if k > 0:
                        prev = xn_keys[k - 1]
                        wait_filled(dve, *prev, 1)
                    if k == 0:
                        dve.wait_ge(pad_ready, 2)
                    mv, r, t0 = (mv1, r1, NT * b) if name == "XT" else (mv2, r2, 0)
                    for t in range(NT):
                        ins = dve.tensor_scalar(xn[:, t, :], X[:, NT * b + t, :],
                                                mv[:, t0 + t, 0:1], r[:, 2, t0 + t:t0 + t + 1],
                                                ALU.subtract, ALU.mult)
                    ins.then_inc(xn_ready, 1)
                elif name == "QP":
                    wait_drained(dve, "QP", b, i, 0)
                    link(dve.tensor_tensor(qf[:, :], qf[:, :], qp[:, 0, :], ALU.subtract))
                    link(dve.tensor_copy(qp[:, 1, :], qf[:, :]))
                    dve.tensor_tensor(qp[:, 2, :], qf[:, :], qp[:, 1, :],
                                      ALU.subtract).then_inc(q_split, 1)
                elif name == "VP":
                    if b >= 2:
                        dve.wait_ge(pv_done, 3 * HG * (b - 1))
                    if b == 1:
                        dve.wait_ge(stack1_const, 1)
                    if b == 0 and i == 0:
                        dve.wait_ge(const_ready, 1)
                    wait_filled(dve, "VP", b, i, 0)
                    pv = bank("VP", b, i, 0)[:, :].rearrange("p (u h d) -> p u h d", u=2, d=HD)
                    for u in range(2):
                        ins = dve.tensor_tensor(
                            Vs[b % 2][:, 2 * i + u, :, 0:HD], pv[:, u],
                            rows[:, 0, :].rearrange("p (h d) -> p h d", d=HD), ALU.add)
                    drain(ins, "VP", b, i, 0)
                elif name == "FT":
                    wait_filled(dve, "FT", 0, 0, 0)
                    drain(dve.tensor_copy(fcol, bank("FT", 0, 0, 0)[:, 0:NB * NT].rearrange(
                        "p (t b) -> p t b", b=NB)), "FT", 0, 0, 0)
                elif name == "CM":
                    dve.wait_ge(cpart_used, NB * S // 256)
                    wait_filled(dve, "SEL", LOW - 1, 3, 0)
                    link(dve.tensor_copy(csum[:, :], OACC[:, :]))
                    dve.tensor_tensor(csum[:, 0:D], csum[:, 0:D], csum[:, D:2 * D],
                                      ALU.add).then_inc(csum_ready, 1)
                    wait_filled(dve, "CM", 0, 0, 0)
                    drain(dve.tensor_copy(cmT, bank("CM", 0, 0, 0)[:, 0:2 * P].rearrange(
                        "p (c b r) -> p c b r", c=KC, b=NB)[:, :, :, 0]), "CM", 0, 0, 0)
                elif name == "VM":
                    wait_filled(dve, "VM", 0, 0, 0)
                    for c in range(KC):
                        ins = dve.tensor_scalar(mvT[:, c, :], bank("VM", 0, 0, 0)[:, NB * c:NB * c + NB],
                                                bv_c[:, c:c + 1], None, ALU.add)
                    drain(ins, "VM", 0, 0, 0)
                elif name == "SM":
                    n = 10 * HG * b + i
                    if n == 0:
                        dve.wait_ge(tri_ready, 1)
                    if b > 0 and i == 0:
                        dve.wait_ge(negmax_ready, b)
                    dve.wait_ge(sm_filled, n + 1)
                    hp, u = divmod(i, 5)
                    h = 2 * hp + (u // 2 if u < 4 else 0)
                    blocks = (((h, 3, 0),) if u in (0, 2) else ((h, 0, 0), (h, 2, P))
                              if u in (1, 3) else ((h, 1, 0), (h + 1, 1, 2 * P)))
                    for hh, qt, at in blocks:
                        w = (qt + 1) * P
                        ins = dve.tensor_tensor_reduce(
                            out=SM[n % SM_RING][:, at:at + w], in0=SM[n % SM_RING][:, at:at + w],
                            in1=tri[:, T - w:T], scale=1.0, scalar=3.0 * NEG, op0=ALU.add,
                            op1=ALU.max, accum_out=rowmax[:, hh, qt:qt + 1])
                    ins.then_inc(max_done, 1)
                elif name == "MR":
                    dve.wait_ge(max_done, 10 * HG * (b + 1))
                    dve.tensor_scalar(negmax, rowmax[:, :, :].rearrange("p h t -> p (h t)"), FLOOR,
                                      -1.0, ALU.max, ALU.mult).then_inc(negmax_ready, 1)
                    if b > 0:
                        dve.wait_ge(maxrow_loaded[b - 1], 48)
                    wait_filled(dve, "MR", b, 0, 0)
                    pm = bank("MR", b, 0, 0)[0:4 * H, 0:P]
                    link(dve.tensor_copy(mparts[:, 0, :], pm))
                    drain(dve.tensor_tensor(mrest[:, :], pm, mparts[:, 0, :], ALU.subtract),
                          "MR", b, 0, 0)
                    wait_drained(dve, "MR", b, 0, 0)
                    link(dve.tensor_copy(mparts[:, 1, :], mrest[:, :]))
                    dve.tensor_tensor(mparts[:, 2, :], mrest[:, :], mparts[:, 1, :],
                                      ALU.subtract).then_inc(mparts_ready, 1)
                elif name == "NM":
                    wait_filled(dve, "NM", b, i, 0)
                    po = bank("NM", b, i, 0)[:, :].rearrange("p (t j c) -> p t j c", t=NT, c=32)
                    link(dve.tensor_scalar(den.rearrange("p (t j) -> p t j", j=4),
                                           po[:, :, :, HD], 1.0e-30, None, ALU.max))
                    link(dve.reciprocal(rden, den))
                    if b > 0 and i == 0:
                        wait_filled(dve, "OT", b - 1, 0, 1)
                    drain(dve.tensor_tensor(
                        On_v[:, :, 64 * i:64 * i + 64].rearrange("p t (j d) -> p t j d", d=HD),
                        po[:, :, :, 0:HD],
                        rden.rearrange("p (t j) -> p t j", j=4).unsqueeze(3).to_broadcast(
                            [P, NT, 4, HD]), ALU.mult), "NM", b, i, 0)
                elif name == "OP":
                    wait_filled(dve, "OP", b, i, 0)
                    dve.wait_ge(base_ready, NT * b + i + 1)
                    xt = X[:, NT * b + i, :]
                    drain(dve.tensor_tensor(xt, bank("OP", b, i, 0)[:, 0:D], xt, ALU.add),
                          "OP", b, i, 0)
                elif name == "F2":
                    wait_filled(dve, "F2", b, i, 0)
                    dve.wait_ge(y_based, NT * b + i + 1)
                    if NT * b + i >= 2:
                        dve.wait_ge(stored[i % 2], 16 * ((NT * b + i) // 2))
                    ins = dve.tensor_tensor(ob[:, i % 2, :], bank("F2", b, i, 0)[:, 0:D],
                                            X[:, NT * b + i, :], ALU.add)
                    drain(ins, "F2", b, i, 0)
                elif name == "EW":
                    wait_filled(dve, "EW", 0, i, 0)
                    drain(dve.tensor_copy(wexpT[:, 2 * i:2 * i + 2, 0:D],
                                          bank("EW", 0, i, 0)[:, :].rearrange(
                                              "p (t c) -> p t c", t=2)), "EW", 0, i, 0)
                    if i == 3:
                        wait_drained(dve, "EW", 0, 3, 0)
                        dve.wait_ge(loaded["cols"], 80)
                        dve.tensor_copy(wexpT[:, :, D], bexp_c).then_inc(wexpT_ready, 1)
                elif name == "SEL":
                    wait_filled(dve, "SEL", b, i, 0)
                    n = 1 << b
                    src = chain_odd if b % 2 else chain_even
                    dst = chain_even if b % 2 else chain_odd
                    pw = bank("SEL", b, i, 0)
                    if b < 5:
                        parts = [(w, 0, NI, 16 * n * w) for w in range(2)]
                    elif b == 5:
                        parts = [(i, 0, NI, 0)]
                    else:
                        parts = [(i // 2, 4 * (i % 2), 4, 0)]
                    for w, t0, nt, at in parts:
                        d = dst[:, w, 0:2 * NI * n].rearrange("p (t a u) -> p t a u", a=2, u=n)[
                            :, t0:t0 + nt]
                        f = pw[:, at:at + 2 * nt * n].rearrange("p (t a u) -> p t a u", a=2, u=n)
                        if b == 0:
                            ins = dve.tensor_copy(d, f)
                        else:
                            s = src[:, w, 0:NI * n].rearrange("p (t u) -> p t u", u=n)[
                                :, t0:t0 + nt].unsqueeze(2).to_broadcast([P, nt, 2, n])
                            ins = dve.tensor_tensor(d, f, s, ALU.mult)
                    drain(ins, "SEL", b, i, 0)
                    wait_drained(dve, "SEL", b, i, 0)
                elif name == "DTR":
                    wait_filled(dve, "DTR", 0, i, 0)
                    drain(dve.tensor_copy(dnT[:, 4 * i:4 * i + 4, :].rearrange("p t j -> p (t j)"),
                                          bank("DTR", 0, i, 0)[:, :]), "DTR", 0, i, 0)
                elif name == "UB":
                    wait_filled(dve, "UB", 0, i, 0)
                    drain(dve.tensor_copy(upY[:, i, :], bank("UB", 0, i, 0)[:, 0:D + 1]),
                          "UB", 0, i, 0)
                elif name == "UST":
                    dve.wait_ge(loaded["stage79"], 16 * 2 * (STAGES - LOW))
                    wait_drained(dve, "UB", 0, NI - 1, 0)
                    ta, tb = up_tmp
                    for e in range(STAGES - LOW):
                        for a in range(NI):
                            if a & (1 << e):
                                continue
                            c = a + (1 << e)
                            g = (a >> (e + 1)) * (1 << e) + a % (1 << e)
                            w = stage79[:, 0, e, g, :]
                            dve.tensor_scalar(ta, upY[:, a, :], w[:, 0:1], None, ALU.mult)
                            link(dve.tensor_scalar(tb, upY[:, a, :], w[:, 2:3], None, ALU.mult))
                            dve.scalar_tensor_tensor(
                                out=upY[:, a, :], in0=upY[:, c, :], scalar=w[:, 1:2], in1=ta,
                                op0=ALU.mult, op1=ALU.add)
                            link(dve.scalar_tensor_tensor(
                                out=upY[:, c, :], in0=upY[:, c, :], scalar=w[:, 3:4], in1=tb,
                                op0=ALU.mult, op1=ALU.add))
                    dve.tensor_tensor(hb, upY[:, :, D], upb_c, ALU.add).then_inc(up_staged, 1)
                elif name == "UT":
                    wait_filled(dve, "UT", 0, i, 0)
                    c, half = divmod(i, 2)
                    drain(dve.tensor_copy(Wu[:, c, 4 * P * half:4 * P * half + 4 * P],
                                          bank("UT", 0, i, 0)[:, :]), "UT", 0, i, 0)
                elif name == "DB":
                    wait_filled(dve, "DB", 0, i, 0)
                    drain(dve.tensor_scalar(
                        Wd[:, 2 * i:2 * i + 2, :].rearrange("p t d -> p (t d)"),
                        bank("DB", 0, i, 0)[:, :], tg[:, 3:4], None, ALU.mult), "DB", 0, i, 0)

        @block.tensor
        def _(pe):
            def take(*key):
                n = turn[key]
                if n >= MISC:
                    pe.wait_ge(drained[n % MISC], n // MISC)
                return MB[n % MISC]

            def fill(ins, *key):
                ins.then_inc(filled[turn[key] % MISC], 1)

            def transposes(blocks, *key):
                dst = take(*key)
                for n, src in enumerate(blocks):
                    ins = pe.transpose(dst[:, P * n:P * n + P], src, ident[:, :])
                fill(ins, *key)

            pe.wait_ge(loaded["ident"], 16)
            for name, b, i in order:
                if name == "WT":
                    pe.wait_ge(loaded["w"], 64)
                    for w in range(4):
                        transposes([wraw[:, w, m, P * c:P * c + P] for c in range(KC)
                                    for m in range(KC)], "WT", 0, 0, w)
                elif name in ("XT", "YT"):
                    pe.wait_ge(xn_ready, xn_turn[(name, b)] + 1)
                    for c in range(KC):
                        transposes([xn[:, t, P * c:P * c + P] for t in range(NT)], name, b, i, c)
                elif name == "CT":
                    pe.wait_ge(ctx_loaded[b], 16)
                    for c in range(KC):
                        transposes([ctxA[:, t, P * c:P * c + P] for t in range(NT)], name, b, i, c)
                elif name in ("QP", "KP"):
                    w, src, key = (0, xnT, "XT") if name == "QP" else (1, ctxT, "CT")
                    if b == 0:
                        wait_drained(pe, "WT", 0, 0, w)
                    wait_drained(pe, key, b, 0, KC - 1)
                    dst = take(name, b, i, 0)
                    for c in range(KC):
                        ins = pe.matmul(dst[:, :], WT[:, w, c, P * i:P * i + P], src[:, c, :],
                                        start=(c == 0), stop=(c == KC - 1))
                    fill(ins, name, b, i, 0)
                elif name == "VP":
                    dst = take(name, b, i, 0)
                    if b == 0:
                        wait_drained(pe, "WT", 0, 0, 2)
                    for u in range(2):
                        kt = 2 * i + u
                        for c in range(KC):
                            ins = pe.matmul(dst[:, D * u:D * u + D], ctxT[:, c, P * kt:P * kt + P],
                                            WT[:, 2, c, :], start=(c == 0), stop=(c == KC - 1))
                    fill(ins, name, b, i, 0)
                elif name == "FT":
                    pe.wait_ge(pad_ready, 2)
                    dst = take(name, b, i, 0)
                    for t in range(NT):
                        ins = pe.transpose(dst[:, NB * t:NB * t + NB], allpad[:, P * t:P * t + P],
                                           ident[0:NB, 0:NB])
                    fill(ins, name, b, i, 0)
                elif name == "CS":
                    n, part = divmod(i, S // 256)
                    if i == 0:
                        pe.wait_ge(const_ready, 1)
                    pe.wait_ge(cpart_loaded[i % 2], 16 * (i // 2 + 1))
                    pe.matmul(OACC[32 * n:32 * n + 32, :], mean32[:, :], cpart[:, i % 2, :],
                              start=(part == 0), stop=(part == S // 256 - 1)).then_inc(cpart_used, 1)
                elif name == "CM":
                    pe.wait_ge(csum_ready, 1)
                    transposes([csum[:, P * c:P * c + P] for c in range(KC)], name, b, i, 0)
                elif name == "VM":
                    wait_drained(pe, "CM", 0, 0, 0)
                    dst = take(name, b, i, 0)
                    for m in range(KC):
                        for c in range(KC):
                            ins = pe.matmul(dst[:, NB * m:NB * m + NB],
                                            WT[:, 2, c, P * m:P * m + P], cmT[:, c, :],
                                            start=(c == 0), stop=(c == KC - 1))
                    fill(ins, name, b, i, 0)
                elif name == "MP":
                    wait_drained(pe, "VM", 0, 0, 0)
                    dst = take(name, b, i, 0)
                    for c in range(KC):
                        ins = pe.matmul(dst[:, 0:D], mvT[:, c, b:b + 1].to_broadcast([P, P]),
                                        WT[:, 3, c, :], start=(c == 0), stop=(c == KC - 1))
                    fill(ins, name, b, i, 0)
                elif name == "EW":
                    if i == 0:
                        pe.wait_ge(loaded["wexp"], 16)
                    transposes([wexp[:, c, P * t:P * t + P] for t in (2 * i, 2 * i + 1)
                                for c in range(KC)], name, b, i, 0)
                elif name == "SEL":
                    if b == 0:
                        pe.wait_ge(loaded["select"], 16)
                        pe.wait_ge(loaded["wlow"], 16 * 2 * (LOW - 1))
                    if b == 6 and i % 2 == 0:
                        pe.wait_ge(loaded["sel6b" if i else "sel6a"], 16)
                    dst = take(name, b, i, 0)
                    n = 1 << b
                    if b < 5:
                        parts = [(wlow_of(b)[:, w], 16 * n * w) for w in range(2)]
                    elif b == 5:
                        parts = [(wlow_of(b)[:, i], 0)]
                    else:
                        parts = [(sel6[:, 4 * (i % 2):4 * (i % 2) + 4, :], 0)]
                    for src, at in parts:
                        v = src.rearrange("q t (u a c) -> q t a u c", a=2, c=2)
                        nt = v.shape[1]
                        for bit in range(2):
                            ins = pe.matmul(dst[:, at:at + 2 * nt * n],
                                            esel[0:64 >> b, 2 * b + bit, :], v[:, :, :, :, bit],
                                            start=(bit == 0), stop=(bit == 1))
                    fill(ins, name, b, i, 0)
                elif name == "DTR":
                    wait_drained(pe, "SEL", LOW - 1, 3, 0)
                    transposes([chain_odd[:, 1, P * t:P * t + P] for t in range(4 * i, 4 * i + 4)],
                               name, b, i, 0)
                elif name == "UB":
                    wait_drained(pe, "EW", 0, 3, 0)
                    if i == 0:
                        pe.wait_ge(wexpT_ready, 1)
                    dst = take(name, b, i, 0)
                    fill(pe.matmul(dst[:, 0:D + 1], chain_odd[:, 0, P * i:P * i + P],
                                   wexpT[:, i, :], start=True, stop=True), name, b, i, 0)
                elif name == "DB":
                    pe.wait_ge(down_staged, 1)
                    wait_drained(pe, "DTR", 0, 1, 0)
                    dst = take(name, b, i, 0)
                    for u in range(2):
                        ins = pe.matmul(dst[:, D * u:D * u + D], dnT[:, 2 * i + u, :],
                                        wcon[:, 2 * i + u, :], start=True, stop=True)
                    fill(ins, name, b, i, 0)
                elif name == "UT":
                    pe.wait_ge(up_staged, 1)
                    c, half = divmod(i, 2)
                    transposes([upY[:, 4 * half + t, P * c:P * c + P] for t in range(4)],
                               name, b, i, 0)
                elif name == "SM":
                    n = 10 * HG * b + i
                    if i == 0:
                        pe.wait_ge(stack_loaded[b], 16 * (2 * len(TERMS) + 1))
                    if n >= SM_RING:
                        pe.wait_ge(max_done, n - SM_RING + 1)
                    hp, u = divmod(i, 5)
                    h = 2 * hp + (u // 2 if u < 4 else 0)
                    blocks = (((h, 3, 0),) if u in (0, 2) else ((h, 0, 0), (h, 2, P))
                              if u in (1, 3) else ((h, 1, 0), (h + 1, 1, 2 * P)))
                    for hh, qt, at in blocks:
                        w = (qt + 1) * P
                        ins = pe.matmul(SM[n % SM_RING][:, at:at + w],
                                        Qs[b % 2][0:KROWS + 1, hh, P * qt:P * qt + P],
                                        Ks[b % 2][0:KROWS + 1, hh, 0:w], start=True, stop=True)
                    ins.then_inc(sm_filled, 1)
                elif name == "MR":
                    pe.wait_ge(negmax_ready, b + 1)
                    dst = take(name, b, i, 0)
                    fill(pe.transpose(dst[0:4 * H, 0:P], negmax, ident[:, :]), name, b, i, 0)
                elif name == "ST":
                    n = 10 * HG * b + i
                    if i == 0:
                        pe.wait_ge(maxrow_loaded[b], 48)
                    if n >= ST_RING:
                        pe.wait_ge(exp_done, n - ST_RING + 1)
                    g, r = divmod(i, 10)
                    blocks = (((4 * g + r, 0, 0),) if r < 4 else
                              ((4 * g + r - 4, 1, 0), (4 * g + r - 4, 3, 3 * P)) if r < 8 else
                              ((4 * g + 2 * (r - 8), 2, 0), (4 * g + 2 * (r - 8) + 1, 2, 2 * P)))
                    for h, kt, at in blocks:
                        w = T - P * kt
                        ins = pe.matmul(ST[n % ST_RING][:, at:at + w],
                                        Ks[b % 2][0:KROWS + 4, h, P * kt:P * kt + P],
                                        Qs[b % 2][0:KROWS + 4, h, P * kt:T], start=True, stop=True)
                    ins.then_inc(st_filled, 1)
                elif name == "PV":
                    g, part = divmod(i, 3)
                    G = HG * b + g
                    n0 = 10 * G
                    if i == 0:
                        wait_drained(pe, "VP", b, 1, 0)
                    if part == 0:
                        pe.wait_ge(oacc_drained, G) if G else pe.wait_ge(csum_ready, 1)
                    pe.wait_ge(mask_done, n0 + (4, 8, 10)[part])
                    for kt in ((0,), (1, 3), (2,))[part]:
                        for j in range(4):
                            n = n0 + (j if part == 0 else 4 + j if part == 1 else 8 + j // 2)
                            at = T * (n % P_RING) + (3 * P if kt == 3 else
                                                     2 * P * (j % 2) if kt == 2 else 0)
                            ins = pe.matmul(OACC[32 * j:32 * j + 32, P * kt:T],
                                            Vs[b % 2][:, kt, 4 * g + j, :],
                                            probs[:, at:at + T - P * kt],
                                            start=(kt == 0), stop=(kt == 2))
                    ins.then_inc(pv_done, 1)
                elif name == "NM":
                    pe.wait_ge(oacc_drained, HG * b + i + 1)
                    transposes([oT[:, (HG * b + i) % 2, P * t:P * t + P] for t in range(NT)],
                               name, b, i, 0)
                elif name == "OT":
                    wait_drained(pe, "NM", b, HG - 1, 0)
                    for c in range(KC):
                        transposes([On_v[:, t, P * c:P * c + P] for t in range(NT)], name, b, i, c)
                elif name == "OP":
                    wait_drained(pe, "OT", b, 0, KC - 1)
                    dst = take(name, b, i, 0)
                    for c in range(KC):
                        ins = pe.matmul(dst[:, 0:D], OnT[:, c, P * i:P * i + P], WT[:, 3, c, :],
                                        start=(c == 0), stop=(c == KC - 1))
                    fill(ins, name, b, i, 0)
                elif name == "F1":
                    wait_drained(pe, "YT", b, 0, KC - 1)
                    if b == 0 and i == 0:
                        wait_drained(pe, "UT", 0, 3, 0)
                    dst = take(name, b, i, 0)
                    for c in range(KC):
                        ins = pe.matmul(dst[:, :], Wu[:, c, P * i:P * i + P], xnT[:, c, :],
                                        start=(c == 0), stop=(c == KC - 1))
                    fill(ins, name, b, i, 0)
                elif name == "F2":
                    wait_drained(pe, "F1", b, NI - 1, 0)
                    if b == 0 and i == 0:
                        wait_drained(pe, "DB", 0, 3, 0)
                    dst = take(name, b, i, 0)
                    for n in range(NI):
                        ins = pe.matmul(dst[:, 0:D], hT[:, n, P * i:P * i + P], Wd[:, n, :],
                                        start=(n == 0), stop=(n == NI - 1))
                    fill(ins, name, b, i, 0)


_INS = ["x", "ctx_1024", "mask_BxS2_bf0", "g_xattn", "g_ffn", "L0_xattn_Wq", "L0_xattn_bq",
        "L0_xattn_Wk", "L0_xattn_bk", "L0_xattn_Wv", "L0_xattn_bv", "L0_xattn_Wo", "L0_xattn_bo",
        "L0_ffn_W_exp", "L0_ffn_b_exp", "L0_ffn_up_weights", "L0_ffn_up_bias",
        "L0_ffn_down_weights", "L0_ffn_W_con", "L0_ffn_b_con", "L0_ffn_down_bias"]


def _constants(NB, T):
    import numpy as np

    j = np.arange(P)
    select = np.zeros((64, 2 * 7, P), np.float32)
    for k in range(7):
        for bit in range(2):
            select[:64 >> k, 2 * k + bit] = (j >> k)[None, :] == 2 * np.arange(64 >> k)[:, None] + bit
    return {"ident": np.eye(P, dtype=np.float32),
            "iota": np.tile(np.arange(T, dtype=np.float32), (NB, 1)), "select": select}


def kernel(**inputs):
    import numpy as _np
    import concourse.bacc as _bacc
    from concourse import mybir as _mybir
    from concourse.bass_utils import run_bass_kernel_spmd as _run

    nc = _bacc.Bacc("TRN2", target_bir_lowering=False, num_devices=1)
    arrays, args = {}, []
    given = [(n, _np.ascontiguousarray(inputs[n])) for n in _INS]
    NB, T, D = given[0][1].shape
    given += list(_constants(NB, T).items())
    for name, a in given:
        arrays[f"in_{name}_dram"] = a
        args.append(nc.dram_tensor(f"in_{name}_dram", a.shape, _mybir.dt.from_np(a.dtype),
                                   kind="ExternalInput").ap())
    args.append(nc.dram_tensor("out_0_dram", (NB, T, D), _mybir.dt.float32,
                               kind="ExternalOutput").ap())
    flamingo_block(nc, *args)
    r = _run(nc, [arrays], core_ids=[0])
    return r.results[0]["out_0_dram"]
```

```python
from contextlib import ExitStack

import concourse.bass as bass
from concourse import mybir

P = 128
F32 = mybir.dt.float32
BF16 = mybir.dt.bfloat16
U8 = mybir.dt.uint8
ALU = mybir.AluOpType
ACT = mybir.ActivationFunctionType
AX_X = mybir.AxisListType.X

NEG = -1.0e30
FLOOR = -1.0e25
EPS = 1.0e-5
MISC = 2
ST_RING = 2
SM_RING = 3
P_RING = 8
LAG = 2
TERMS = ((0, 0), (0, 1), (0, 2), (1, 0), (1, 1), (2, 0))
TERM_RUNS = ((0, 3), (3, 2), (5, 1))


COST = {"ST": 2, "SM": 1.5, "PV": 5, "NM": 2, "WT": 4, "XT": 8, "YT": 8, "CT": 8, "OT": 8,
        "QP": 8, "KP": 8, "VP": 8, "OP": 4, "F1": 5.6, "F2": 16, "EW": 4, "SEL": 6, "DTR": 4,
        "UB": 3, "DB": 4, "UT": 4, "MP": 4}
USES = {"WT": 1, "XT": 2, "YT": 2, "CT": 2, "OT": 2, "QP": 1, "KP": 1, "VP": 1, "FT": 1, "EW": 1,
        "SEL": 1, "DTR": 1, "UB": 1, "DB": 1, "UT": 1, "CM": 1, "VM": 1, "MP": 1, "MR": 1, "NM": 1,
        "OP": 1, "F1": 1, "F2": 1}


def weave(*lists):
    placed = []
    for w, items in enumerate(lists):
        costs = [sum(COST.get(s[0], 0.5) for s in (x if isinstance(x, list) else [x]))
                 for x in items]
        at = 0.0
        for x, c in zip(items, costs):
            placed.append(((at + c / 2) / sum(costs), w, len(placed), x))
            at += c
    return [p[-1] for p in sorted(placed, key=lambda p: p[:3])]


def flat(items):
    return [s for x in items for s in (x if isinstance(x, list) else [x])]


def attention(b, HG):
    out = []
    for g in range(HG):
        for r in range(10):
            out.append(("ST", b, 10 * g + r))
            if r == 1 and g:
                out.append(("PV", b, 3 * g - 1))
            elif r == 3 and g:
                out.append(("NM", b, g - 1))
            elif r in (5, 9):
                out.append(("PV", b, 3 * g + (r == 9)))
    return out + [("PV", b, 3 * HG - 1), ("NM", b, HG - 1)]


def plan(NB, HG, NT, NI, LOW):

    def steps(name, b, count):
        return [(name, b, i) for i in range(count)]

    def scores_for_max(b):
        half = 5 * HG
        units = steps("SM", b, 2 * half)
        return (units[:half] + [("MX", b, 0)] + units[half:half + LAG] + [("MR", b, 0)] +
                units[half + LAG:] + [("MX", b, 1)])

    sel = [("SEL", k, u) for k in range(LOW) for u in range(1 if k < 5 else 2 if k == 5 else 4)]
    order = [("LN1", 0, 0), ("LNS", 0, 0), ("WT", 0, 1), ("WT", 0, 0), ("CT", 0, 0), ("XN", 0, 0),
             ("XT", 0, 0), ("KP", 0, 0), ("QP", 0, 0), ("PAD", 0, 0), ("STK", 0, 0)]
    order += steps("EW", 0, 4) + sel[:4]
    order += [("KP", 0, 1), ("QP", 0, 1), ("STK", 0, 1), ("FT", 0, 0), ("GATE", 0, 0)]
    prep = [("DSP", 0, 0), ("WT", 0, 2), ("WT", 0, 3), ("ROWS", 0, 0), ("VP", 0, 0), ("VP", 0, 1),
            ("KS", 0, 0), ("KS", 0, 1)]
    prep += [("KS", 0, 2), ("KS", 0, 3)] + sel[4:9]
    dst = steps("DST", 0, NI)
    for k in range(NI // 2):
        prep += [dst[k]] + sel[9 + k:10 + k]
    prep += sel[9 + NI // 2:] + steps("DTR", 0, 2)
    order += weave(scores_for_max(0), prep) + steps("CS", 0, NB)
    order += [("CM", 0, 0), ("MR", 0, 1), ("VM", 0, 0), ("LN1", 1, 0)]
    for b in range(NB + 1):
        maxima = []
        if b + 1 < NB:
            n = b + 1
            project = [("XT", n, 0), ("CT", n, 0), ("KP", n, 0), ("QP", n, 0), ("KP", n, 1),
                       ("QP", n, 1)]
            stack, values = steps("STK", n, 2), steps("VP", n, 2)
            maxima = weave(scores_for_max(n), steps("BASE", n, NT))
            if n + 1 < NB:
                maxima.insert(-4, ("XN", n + 1, 0))
        if b >= 1:
            n = b - 1
            f1 = steps("F1", n, NI)
            f2 = steps("F2", n, NT)
            behind = [("OT", n, 0)] + steps("OP", n, NT) + [("LN2", n, 0), ("YT", n, 0)]
        if b == 0:
            ust = steps("UST", 0, 3 * NI // 2)
            first = (steps("UB", 0, NI // 2) + [("LNS", 1, 0), ("XN", 1, 0)] +
                     steps("UB", 0, NI)[NI // 2:] + project[:2] + weave(project[2:], ust[:NI]) +
                     [("C1", 0, 0)] + weave(values + steps("MP", 0, 2), ust[NI:]) +
                     steps("UT", 0, 4) + stack +
                     weave([("MP", 0, n) for n in range(2, NB)], dst[NI // 2:]) +
                     steps("DB", 0, 4) + steps("BASE", 0, NT))
            second = maxima
        elif b + 1 < NB:
            ot, op, ln2, yt = behind[:1], behind[1:-2], behind[-2:-1], behind[-1:]
            first = (project[:1] + ot + project[1:4] + op[:1] + stack[:1] + project[4:5] +
                     op[1:] + ln2 + project[5:] + stack[1:] + values + yt)
            if b >= 2:
                first = weave(first, steps("F2", b - 2, NT))
            n = len(maxima)
            cut = [n // 8, n // 4, 9 * n // 16]
            second = (maxima[:cut[0]] + [f1[:NI // 2]] + maxima[cut[0]:cut[1]] +
                      [flat(weave(maxima[cut[1]:cut[2]], f1[NI // 2:]))] + maxima[cut[2]:])
        elif b < NB:
            first = weave(behind, steps("F2", b - 2, NT))
            second = [f1[:NI // 2], f1[NI // 2:]] + f2[:NT // 2]
        else:
            first = behind[:-1] + steps("F2", b - 2, NT)[NT // 2:] + behind[-1:]
            second = f1 + f2
        if 1 <= b < NB:
            first.insert(1, ("MR", b, 1))
        fill = first + second
        order += flat(weave(attention(b, HG), fill) if b < NB else fill)
    turn, n = {}, 0
    for name, b, i in order:
        for j in range(USES.get(name, 0)):
            turn[(name, b, i, j)] = n
            n += 1
    return order, turn


def flamingo_block(nc, x, ctx_in, mask, g_xattn, g_ffn, Wq, bq, Wk, bk, Wv, bv, Wo, bo,
                   W_exp, b_exp, up_w, up_b, dn_w, W_con, b_con, dn_b, ident_in, iota_in,
                   select_in, out):
    NB, T, D = x.shape
    S = ctx_in.shape[1]
    H, HD = 16, D // 16
    NT = T // P
    KC = D // P
    NH = W_exp.shape[1]
    NI = NH // P
    STAGES = up_w.shape[0]
    LOW = 7
    HG = H // 4
    PAIRS = NI // 2
    KROWS = 16 * len(TERMS)
    SCALE = float(HD) ** -0.5
    assert (T, D, NH, STAGES, HD) == (512, 256, 1024, 10, 16)

    order, turn = plan(NB, HG, NT, NI, LOW)

    with ExitStack() as ctx:
        def sb(name, shape, dt=F32):
            return ctx.enter_context(nc.sbuf_tensor(name, shape, dt))

        def ps(name, shape=(P, 512), dt=F32):
            return ctx.enter_context(nc.psum_tensor(name, list(shape), dt))

        def sem(name):
            return ctx.enter_context(nc.semaphore(name))

        ST = [ps(f"ps_st{i}") for i in range(ST_RING)]
        SM = [ps(f"ps_sm{i}") for i in range(SM_RING)]
        OACC = ps("ps_oacc")
        MB = [ps(f"ps_misc{i}") for i in range(MISC)]

        ident = sb("ident", [P, P])
        tri = sb("tri", [P, T], BF16)
        stack0 = sb("stack0", [P, 2 * 4096])
        stack1 = sb("stack1", [P, 2 * 4096])
        X = sb("X", [P, NB * NT, D])
        xn = sb("xn", [P, NT, D])
        xnT = sb("xnT", [P, KC, T])
        ctxA = sb("ctxA", [P, NT, D])
        ctxT = sb("ctxT", [P, KC, T])
        qf, kf = sb("qf", [P, T]), sb("kf", [P, T])
        qp, kp = sb("qp", [P, 3, T], BF16), sb("kp", [P, 3, T], BF16)
        Vs = [sb(f"Vs{i}", [P, NT, H, 32]) for i in range(2)]
        probs = sb("probs", [P, P_RING * T])
        oT = sb("oT", [P, 2, T])
        On = sb("On", [P, 2 * 1024])
        Wu = sb("Wu", [P, KC, NH])
        Wd = sb("Wd", [P, NI, D])
        hT = sb("hT", [P, NI, T])
        WT = sb("WT", [P, 4, KC, D])
        rows = sb("rows", [P, 3, D])
        mp = sb("mp", [P, NB, D])
        ob = sb("ob", [P, 2, D])
        cols = sb("cols", [P, 64])
        small = sb("small", [P, 512 // 4])
        rowmax = sb("rowmax", [P, H, NT])
        mparts = sb("mparts", [2 * H, 2, 3, P], BF16)
        pool_tmp = sb("pool_tmp", [P, 2, D])
        mrest = sb("mrest", [2 * H, P])
        nokey = sb("nokey", [P, 2 * H])
        tg = sb("tg", [P, 4])
        mean32 = sb("mean32", [P, 32])
        stage79 = sb("stage79", [P, 2, 3, 4, 4])
        lnst = sb("lnst", [P, NT, 6])
        mv1 = sb("mv1", [P, NB * NT, 2])
        r1 = sb("r1", [P, 4, NB * NT])
        mv2 = sb("mv2", [P, NT, 2])
        r2 = sb("r2", [P, 4, NT])
        rowsrc = sb("rowsrc", [35, T], BF16)

        bq_c, bk_c, bv_c = cols[:, 0:2], cols[:, 2:4], cols[:, 4:6]
        upb_c, bexp_c, hb = cols[:, 8:16], cols[:, 16:24], cols[:, 24:32]
        fcol = cols[:, 32:48].rearrange("p (t b) -> p t b", b=NB)
        cmT = small[:, 0:8].rearrange("p (c b) -> p c b", b=NB)
        mvT = small[:, 8:16].rearrange("p (c b) -> p c b", b=NB)
        negmax = small[:, 32:96]
        den = small[:, 96:112]
        rden = small[:, 112:128]

        def stacks(buf):
            v = buf[:, :].bitcast(BF16).rearrange("p (w h t) -> p w h t", w=2, t=T)
            return v[:, 0], v[:, 1]

        Qs, Ks = zip(*(stacks(s) for s in (stack0, stack1)))

        padb, ones = rowsrc[0:NB, :], rowsrc[32:35, :]

        wexp = stack1[:, 0:2048].rearrange("p (c n) -> p c n", c=KC)
        dnT = hT[:, 0:2, :].rearrange("p a (t j) -> p (a t) j", j=P)
        down_tmp = [ob[:, 0, :], ob[:, 1, :]]
        csum = stack1[:, 1536:1536 + D]
        chain_odd = stack1[:, 2048:4096].rearrange("p (w n) -> p w n", w=2)
        chain_even = stack1[:, 4096:5120].rearrange("p (w n) -> p w n", w=2)
        upY = stack1[:, 5120:5120 + NI * (D + 1)].rearrange("p (t c) -> p t c", c=D + 1)
        up_tmp = [stack1[:, 7176:7176 + D + 1], stack1[:, 7434:7434 + D + 1]]
        wlow = hT[:, :, :].rearrange("p t n -> p (t n)")
        wlow6 = hT[64:65, :, :].rearrange("o t n -> o (t n)").rearrange("o (w t n) -> o w t n", w=2,
                                                                        t=NI)
        esel = Vs[1][0:65].rearrange("p t h c -> p (t h c)")[:, 0:2 * LOW * P].rearrange(
            "p (s m) -> p s m", m=P)
        wraw = On[:, 0:2048].rearrange("p (w m c) -> p w m c", w=4, c=D)
        all_keys = [probs[:, 4 * T * k:4 * T * (k + 1)] for k in range(2)]
        pad_u8 = oT[0:NB, 0, 0:T // 4].bitcast(U8)
        keys_sum = oT[:, :, :].rearrange("p a (n d) -> p (a n) d", d=D)
        scratch = nc.dram_tensor("qk_parts", (NB, 2, 3, HD, H, T), BF16, kind="Internal").ap()
        padf, iota, padt, allpad = (probs[0:NB, 4 * T + T * k:4 * T + T * k + T] for k in range(4))
        first_key = cols[0:NB, 48:49]

        On_v = On[:, 0:1024].rearrange("p (t n) -> p t n", n=D)
        OnT = On[:, 1024:2048].rearrange("p (c n) -> p c n", c=KC)

        def wlow_of(k):
            if k == LOW - 1:
                return wlow6
            n = 64 << k
            off = 64 * ((1 << k) - 1)
            return wlow[0:64 >> k, off:off + n].rearrange("p (w t n) -> p w t n", w=2, t=NI)

        loaded = {n: sem("ld_" + n) for n in
                  ("ident", "w0", "w1", "w2", "w3", "rows", "cols", "cols2", "mask",
                   "select", "wexp", "wcon", "wlow",
                   "stage79", "gate", "ones0", "ones1")}
        x_loaded = [sem(f"x_loaded{b}") for b in range(NB)]
        ctx_loaded = [sem(f"ctx_loaded{b}") for b in range(NB)]
        keys_loaded = [sem(f"keys_loaded{i}") for i in range(NB)]
        q_written = [sem(f"q_written{b}") for b in range(NB)]
        k_written = [sem(f"k_written{b}") for b in range(NB)]
        stack_loaded = [[sem(f"stack_loaded{b}_{i}") for i in range(2)] for b in range(NB)]
        maxrow_loaded = [[sem(f"maxrow_loaded{b}_{i}") for i in range(2)] for b in range(NB)]
        stored = [sem(f"stored{i}") for i in range(2)]
        filled = [sem(f"misc_filled{i}") for i in range(MISC)]
        drained = [sem(f"misc_drained{i}") for i in range(MISC)]
        st_filled, exp_done, mask_done = sem("st_filled"), sem("exp_done"), sem("mask_done")
        pv_done, oacc_drained = sem("pv_done"), sem("oacc_drained")
        sm_filled, max_done = sem("sm_filled"), sem("max_done")
        q_split, k_split = sem("q_split"), sem("k_split")
        xn_ready, var_ready, std_ready = sem("xn_ready"), sem("var_ready"), sem("std_ready")
        base_ready, y_based, up_staged = sem("base_ready"), sem("y_based"), sem("up_staged")
        keys_added, keys_summed = sem("keys_added"), sem("keys_summed")
        pad_ready, const_ready = sem("pad_ready"), sem("const_ready")
        negmax_ready, mparts_ready = sem("negmax_ready"), sem("mparts_ready")
        tanh_ready, csum_ready, down_staged = sem("tanh_ready"), sem("csum_ready"), sem("down_staged")
        value_const, wexpT_ready = sem("value_const"), sem("wexpT_ready")
        down_top_staged, ones_ready = sem("down_top_staged"), sem("ones_ready")
        tri_ready = sem("tri_ready")
        dve_step, pool_step = sem("dve_step"), sem("pool_step")

        def bank(*key):
            return MB[turn[key] % MISC]

        def wait_filled(eng, *key):
            eng.wait_ge(filled[turn[key] % MISC], turn[key] // MISC + 1)

        def wait_drained(eng, *key):
            eng.wait_ge(drained[turn[key] % MISC], turn[key] // MISC + 1)

        def drain(ins, *key):
            ins.then_inc(drained[turn[key] % MISC], 1)

        xn_turn = {s[:2]: n for n, s in enumerate(s for s in order if s[0] in ("XT", "YT"))}
        xn_keys = [s for s in order if s[0] in ("XT", "YT")]

        def last_reader_of_xnT(k):
            name, b, _ = xn_keys[k]
            return ("QP", b, 1, 0) if name == "XT" else ("F1", b, NI - 1, 0)

        def pairs(e, w):
            for a in range(NI):
                if not a & (1 << e):
                    g = (a >> (e + 1)) * (1 << e) + a % (1 << e)
                    yield a, a + (1 << e), stage79[:, w, e, g, :]

        def burst_of(n):
            return 3 * (n // 10) + (0 if n % 10 < 4 else 1 if n % 10 < 8 else 2)

        block = ctx.enter_context(nc.Block())

        @block.sync
        def _(sp):
            def load(name, dst, src):
                sp.dma_start(dst, src).then_inc(loaded[name], 16)

            load("ident", ident[:, :], ident_in)

            def load_x(b):
                sp.dma_start(X[:, NT * b:NT * b + NT, :],
                             x[b].rearrange("(i p) d -> p i d", p=P)).then_inc(x_loaded[b], 16)

            load_x(0)
            sp.dma_start(ctxA[:, :, :], ctx_in[0, 0:T].rearrange("(i p) d -> p i d", p=P)
                         ).then_inc(ctx_loaded[0], 16)
            load("mask", pad_u8, mask[:, 0:T])
            load("mask", iota, iota_in)
            for i, r in enumerate((bv, bo, b_con)):
                load("rows", rows[:, i, :], r.partition_broadcast(P))
            load("rows", ob[:, 0, :], dn_b.partition_broadcast(P))
            load("wcon", Wd[:, :, :], W_con.rearrange("(t p) d -> p t d", p=P))
            load("wexp", wexp, W_exp.rearrange("(c p) n -> p c n", p=P))
            load("select", esel, select_in)
            for k in range(LOW):
                for w, src in enumerate((up_w, dn_w)):
                    load("wlow", wlow_of(k)[:, w],
                         src[k].rearrange("(t q u) a c -> q t (u a c)", t=NI, u=1 << k))

            def load_keys(n):
                sp.dma_start(all_keys[n % 2].rearrange("p (r d) -> p r d", d=D),
                             ctx_in[n].rearrange("(p r) d -> p r d", p=P)
                             ).then_inc(keys_loaded[n], 16)

            stores = 0
            for name, b, i in order:
                if name in ("QP", "KP"):
                    parts, split, done, w = ((qp, q_split, q_written, 0) if name == "QP" else
                                             (kp, k_split, k_written, 1))
                    sp.wait_ge(split, 2 * b + i + 1)
                    heads = slice(H // 2 * i, H // 2 * (i + 1))
                    for s in range(3):
                        sp.dma_start(scratch[b, w, s, :, heads].rearrange("d h t -> h d t"),
                                     parts[:, s, :]).then_inc(done[b], 16)
                elif name == "VP" and i == 1 and b + 1 < NB:
                    wait_filled(sp, "CT", b, 0, 1)
                    sp.dma_start(ctxA[:, :, :], ctx_in[b + 1, 0:T].rearrange("(i p) d -> p i d", p=P)
                                 ).then_inc(ctx_loaded[b + 1], 16)
                elif name == "STK":
                    if i == 0:
                        if b >= 2:
                            sp.wait_ge(st_filled, 10 * HG * (b - 1))
                        if b == 1:
                            wait_filled(sp, "DTR", 0, 1, 0)
                            wait_filled(sp, "UT", 0, 3, 0)
                            wait_filled(sp, "CM", 0, 0, 0)
                        if b < 2:
                            sp.wait_ge(ones_ready, 1)
                            load(f"ones{b}", Ks[b][KROWS + 1:KROWS + 4, :, :],
                                 ones.unsqueeze(1).to_broadcast([3, H, T]))
                            load(f"ones{b}", Qs[b][KROWS:KROWS + 1, :, :],
                                 ones[0:1].unsqueeze(1).to_broadcast([1, H, T]))
                        sp.wait_ge(pad_ready, 1)
                        sp.dma_start(Ks[b % 2][KROWS:KROWS + 1, :, :],
                                     padb[b:b + 1, :].unsqueeze(1).to_broadcast([1, H, T])
                                     ).then_inc(stack_loaded[b][0], 16)
                    sp.wait_ge(q_written[b], 48 * (i + 1))
                    sp.wait_ge(k_written[b], 48 * (i + 1))
                    heads = slice(H // 2 * i, H // 2 * (i + 1))
                    for part, (r, n) in enumerate(TERM_RUNS):
                        sp.dma_start(Qs[b % 2][HD * r:HD * (r + n), heads, :].rearrange(
                            "p h t -> p (h t)"),
                            scratch[b, 0, part, :, heads].rearrange("d h t -> d (h t)").unsqueeze(0)
                            .to_broadcast([n, HD, H // 2 * T])).then_inc(stack_loaded[b][i], 16)
                        sp.dma_start(Ks[b % 2][HD * r:HD * (r + n), heads, :].rearrange(
                            "p h t -> p (h t)"),
                            scratch[b, 1, 0:n, :, heads].rearrange("s d h t -> (s d) (h t)")
                            ).then_inc(stack_loaded[b][i], 16)
                elif name == "MR":
                    sp.wait_ge(mparts_ready, 2 * b + i + 1)
                    for s in range(3):
                        sp.dma_start(Qs[b % 2][KROWS + 1 + s:KROWS + 2 + s,
                                               H // 2 * i:H // 2 * (i + 1), :].rearrange(
                            "p h t -> p (h t)"), mparts[:, i, s, :]).then_inc(maxrow_loaded[b][i], 16)
                elif name == "FT":
                    for w in range(1, NB):
                        load_x(w)
                    wait_filled(sp, "FT", 0, 0, 0)
                    for w in range(2):
                        load_keys(w)
                elif name == "KS" and i + 2 < NB:
                    sp.wait_ge(keys_added, i + 1)
                    load_keys(i + 2)
                elif name == "F2":
                    wait_drained(sp, "F2", b, i, 0)
                    sp.dma_start(out[b, P * i:P * i + P, :], ob[:, i % 2, :]).then_inc(
                        stored[i % 2], 16)
                    stores += 1
            for s in stored:
                sp.wait_ge(s, 16 * (stores // 2))

        @block.gpsimd
        def _(pool):
            steps = [0]

            def link(ins):
                steps[0] += 1
                ins.then_inc(pool_step, 1)
                pool.wait_ge(pool_step, steps[0])

            link(pool.memset(tri[:, :], 0.0))
            pool.affine_select(out=tri[:, T - P:T], in_=tri[:, T - P:T], compare_op=ALU.is_ge,
                               fill=NEG, base=0, pattern=[[-1, P]],
                               channel_multiplier=1).then_inc(tri_ready, 1)
            link(pool.memset(mean32[:, :], 1.0 / S))
            pool.memset(ones, 1.0).then_inc(ones_ready, 1)
            pool.wait_ge(ones_ready, 1)
            link(pool.memset(Vs[0][:, :, :, HD:32], 0.0))
            pool.memset(Vs[0][:, :, :, HD:HD + 1], 1.0).then_inc(const_ready, 1)
            pool.wait_ge(const_ready, 1)

            def load(name, dst, src, slow=False):
                pool.dma_start(dst, src, allow_slow_non_contiguous=slow).then_inc(loaded[name], 16)

            for src, dst in ((bk, bk_c), (bq, bq_c)):
                load("cols", dst, src.rearrange("(c p) -> p c", p=P), True)
            load("gate", tg[:, 0:1], g_xattn.partition_broadcast(P))
            load("gate", tg[:, 1:2], g_ffn.partition_broadcast(P))
            for i, w in ((2, Wv), (3, Wo)):
                load(f"w{i}", wraw[:, i], w.rearrange("(m p) c -> p m c", p=P))
            for w, src in enumerate((up_w, dn_w)):
                for e in range(STAGES - LOW):
                    load("stage79", stage79[:, w, e],
                         src[LOW + e].rearrange("(g p) a c -> p g (a c)", p=P))
            for src, dst in ((bv, bv_c), (up_b, upb_c), (b_exp, bexp_c)):
                load("cols2", dst, src.rearrange("(c p) -> p c", p=P), True)

            for name, b, i in order:
                if name == "KS":
                    pool.wait_ge(keys_loaded[i], 16)
                    keys = all_keys[i % 2]
                    if i == 0:
                        pool.wait_ge(pad_ready, 1)
                    for n in (4 * D, 2 * D):
                        link(pool.tensor_tensor(keys[:, 0:n], keys[:, 0:n], keys[:, n:2 * n],
                                                ALU.add))
                    pool.tensor_tensor(keys_sum[:, i, :], keys[:, 0:D], keys[:, D:2 * D],
                                       ALU.add).then_inc(keys_added, 1)
                    pool.wait_ge(keys_added, i + 1)
                elif name == "DSP":
                    pool.wait_ge(loaded["wcon"], 16)
                    pool.wait_ge(loaded["stage79"], 16 * 2 * (STAGES - LOW))
                    pool.wait_ge(tanh_ready, 2)
                    ta, tb, tc = ob[:, 1, :], pool_tmp[:, 1, :], pool_tmp[:, 0, :]
                    for a, c, w in pairs(STAGES - LOW - 1, 1):
                        pool.tensor_scalar(ta, Wd[:, a, :], w[:, 0:1], None, ALU.mult)
                        link(pool.tensor_scalar(tb, Wd[:, a, :], w[:, 1:2], None, ALU.mult))
                        link(pool.tensor_scalar(tc, Wd[:, c, :], w[:, 2:3], None, ALU.mult))
                        link(pool.tensor_scalar(Wd[:, c, :], Wd[:, c, :], w[:, 3:4],
                                                None, ALU.mult))
                        pool.tensor_tensor(Wd[:, a, :], tc, ta, ALU.add)
                        ins = pool.tensor_tensor(Wd[:, c, :], Wd[:, c, :], tb, ALU.add)
                        if c < NI - 1:
                            link(ins)
                    ins.then_inc(down_top_staged, 1)
                    pool.wait_ge(down_top_staged, 1)
                elif name == "BASE":
                    if b == 0 and i == 0:
                        pool.wait_ge(tanh_ready, 2)
                        wait_drained(pool, "FT", 0, 0, 0)
                    if i == 0:
                        pool.wait_ge(xn_ready, xn_turn[("XT", b)] + 1)
                        wait_drained(pool, "MP", 0, b, 0)
                    n = NT * b + i
                    xt = X[:, n, :]
                    pool.tensor_tensor(xt, xt, rows[:, 1, :], ALU.add)
                    tmp = pool_tmp[:, n % 2, :]
                    if n >= 2:
                        pool.wait_ge(base_ready, n - 1)
                    link(pool.tensor_scalar(tmp, mp[:, b, :], fcol[:, i, b:b + 1], None, ALU.mult))
                    pool.tensor_tensor(xt, xt, tmp, ALU.add).then_inc(base_ready, 1)
                elif name == "C1":
                    wait_filled(pool, "SEL", LOW - 1, 3, 0)
                    link(pool.memset(Vs[1][:, :, :, HD:32], 0.0))
                    pool.memset(Vs[1][:, :, :, HD:HD + 1], 1.0).then_inc(value_const, 1)
                    pool.wait_ge(value_const, 1)
                elif name == "ST":
                    n = 10 * HG * b + i
                    pool.wait_ge(exp_done, n + 1)
                    p = probs[:, T * (n % P_RING):T * (n % P_RING) + T]
                    r = i % 10
                    step = T if r < 4 else 3 * P if r < 8 else 2 * P
                    v = (p[:, 0:P].unsqueeze(1) if r < 4 else
                         p.rearrange("p (n c) -> p n c", c=P)[:, 0::step // P, :])
                    nblk = 1 if r < 4 else 2
                    pool.affine_select(out=v, in_=v, compare_op=ALU.is_ge, fill=0.0, base=0,
                                       pattern=[[0, nblk], [1, P]],
                                       channel_multiplier=-1).then_inc(mask_done, 1)
                elif name == "YT":
                    pool.wait_ge(xn_ready, xn_turn[("YT", b)] + 1)
                    for t in range(NT):
                        xt = X[:, NT * b + t, :]
                        pool.tensor_tensor(xt, xt, rows[:, 2, :], ALU.add).then_inc(y_based, 1)

        @block.scalar
        def _(act):
            for i, w in ((1, Wk), (0, Wq)):
                act.dma_start(wraw[:, i], w.rearrange("(m p) c -> p m c", p=P)).then_inc(
                    loaded[f"w{i}"], 16)
            for name, b, i in order:
                if name == "LNS":
                    act.wait_ge(var_ready, b + 1)
                    t0, t1 = (0, NT) if b == 0 else (NT, NB * NT)
                    act.activation(r1[:, 1, t0:t1], r1[:, 0, t0:t1],
                                   ACT.Sqrt).then_inc(std_ready, 1)
                elif name == "LN2":
                    act.wait_ge(var_ready, b + 3)
                    act.activation(r2[:, 1, :], r2[:, 0, :], ACT.Sqrt).then_inc(std_ready, 1)
                elif name == "GATE":
                    act.wait_ge(loaded["gate"], 32)
                    act.activation(tg[:, 2:4], tg[:, 0:2], ACT.Tanh).then_inc(tanh_ready, 1)
                elif name == "WT" and i < 3:
                    wait_filled(act, "WT", 0, i, 0)
                    drain(act.copy(WT[:, i].rearrange("p c n -> p (c n)"),
                                   bank("WT", 0, i, 0)[:, :]), "WT", 0, i, 0)
                elif name == "EW":
                    wait_filled(act, "EW", 0, i, 0)
                    drain(act.copy(upY[:, 2 * i:2 * i + 2, 0:D],
                                   bank("EW", 0, i, 0)[:, :].rearrange("p (t c) -> p t c", t=2)),
                          "EW", 0, i, 0)
                elif name == "DTR":
                    wait_filled(act, "DTR", 0, i, 0)
                    drain(act.copy(dnT[:, 4 * i:4 * i + 4, :].rearrange("p t j -> p (t j)"),
                                   bank("DTR", 0, i, 0)[:, :]), "DTR", 0, i, 0)
                elif name == "UB":
                    wait_filled(act, "UB", 0, i, 0)
                    drain(act.copy(upY[:, i, :], bank("UB", 0, i, 0)[:, 0:D + 1]), "UB", 0, i, 0)
                elif name == "UT":
                    wait_filled(act, "UT", 0, i, 0)
                    c, half = divmod(i, 2)
                    drain(act.copy(Wu[:, c, 4 * P * half:4 * P * half + 4 * P],
                                   bank("UT", 0, i, 0)[:, :]), "UT", 0, i, 0)
                elif name == "DB":
                    wait_filled(act, "DB", 0, i, 0)
                    drain(act.activation(
                        Wd[:, 2 * i:2 * i + 2, :].rearrange("p t d -> p (t d)"),
                        bank("DB", 0, i, 0)[:, :], ACT.Copy, scale=tg[:, 3:4]), "DB", 0, i, 0)
                elif name in ("XT", "YT", "CT", "OT"):
                    dst = {"CT": ctxT, "OT": OnT}.get(name, xnT)
                    if name in ("XT", "YT") and xn_turn[(name, b)] > 0:
                        wait_filled(act, *last_reader_of_xnT(xn_turn[(name, b)] - 1))
                    if name == "CT" and b > 0:
                        wait_filled(act, "KP", b - 1, 1, 0)
                        wait_filled(act, "VP", b - 1, 1, 0)
                    if name == "OT" and b > 0:
                        wait_filled(act, "OP", b - 1, NT - 1, 0)
                    for c in range(KC):
                        wait_filled(act, name, b, i, c)
                        drain(act.copy(dst[:, c, :], bank(name, b, i, c)[:, :]), name, b, i, c)
                elif name in ("QP", "KP"):
                    f, parts, bias, split, done = ((qf, qp, bq_c, q_split, q_written)
                                                   if name == "QP" else
                                                   (kf, kp, bk_c, k_split, k_written))
                    n = 2 * b + i
                    if n > 0:
                        act.wait_ge(split, n)
                        act.wait_ge(done[(n - 1) // 2], 48 * ((n - 1) % 2 + 1))
                    act.wait_ge(loaded["cols"], 32)
                    wait_filled(act, name, b, i, 0)
                    pq = bank(name, b, i, 0)
                    act.activation(f[:, :], pq[:, :], ACT.Identity, bias=bias[:, i:i + 1])
                    drain(act.activation(parts[:, 0, :], pq[:, :], ACT.Identity,
                                         bias=bias[:, i:i + 1]), name, b, i, 0)
                elif name == "MP":
                    wait_filled(act, "MP", 0, i, 0)
                    drain(act.copy(mp[:, i, :], bank("MP", 0, i, 0)[:, 0:D]), "MP", 0, i, 0)
                elif name == "ST":
                    n = 10 * HG * b + i
                    if n >= P_RING:
                        act.wait_ge(pv_done, burst_of(n - P_RING) + 1)
                    if n == 0:
                        act.wait_ge(keys_added, NB)
                    act.wait_ge(st_filled, n + 1)
                    act.activation(probs[:, T * (n % P_RING):T * (n % P_RING) + T],
                                   ST[n % ST_RING][:, :], ACT.Exp, scale=SCALE).then_inc(exp_done, 1)
                elif name == "PV" and i % 3 == 2:
                    G = HG * b + i // 3
                    act.wait_ge(pv_done, 3 * (G + 1))
                    if G == 0:
                        act.wait_ge(keys_summed, NB)
                    if G >= 2:
                        wait_filled(act, "NM", (G - 2) // HG, (G - 2) % HG, 0)
                    act.copy(oT[:, G % 2, :], OACC[:, :]).then_inc(oacc_drained, 1)
                elif name == "F1":
                    if b == 0:
                        wait_filled(act, "DB", 0, 3, 0)
                    else:
                        wait_filled(act, "F2", b - 1, NT - 1, 0)
                    wait_filled(act, "F1", b, i, 0)
                    act.wait_ge(up_staged, 1)
                    drain(act.activation(hT[:, i, :], bank("F1", b, i, 0)[:, :], ACT.Gelu,
                                         bias=hb[:, i:i + 1]), "F1", b, i, 0)

        @block.vector
        def _(dve):
            steps = [0]

            def link(ins):
                steps[0] += 1
                ins.then_inc(dve_step, 1)
                dve.wait_ge(dve_step, steps[0])

            def inverse_std(r, t0, t1):
                var, root, inv, tmp = (r[:, k, t0:t1] for k in range(4))
                link(dve.reciprocal(inv, root))
                link(dve.tensor_tensor(tmp, inv, inv, ALU.mult))
                link(dve.tensor_tensor(tmp, tmp, var, ALU.mult))
                link(dve.tensor_scalar(tmp, tmp, -0.5, 1.5, ALU.mult, ALU.add))
                link(dve.tensor_tensor(inv, inv, tmp, ALU.mult))

            for name, b, i in order:
                if name == "LN1":
                    t0, t1 = (0, NT) if b == 0 else (NT, NB * NT)
                    for t in range(t0, t1):
                        if t % NT == 0:
                            dve.wait_ge(x_loaded[t // NT], 16)
                        ins = dve.bn_stats(lnst[:, t % NT, :], X[:, t, :])
                        if t % NT == NT - 1:
                            link(ins)
                            for k in range(NT):
                                ins = dve.bn_aggr(mv1[:, t + 1 - NT + k, :], lnst[:, k, :])
                            link(ins)
                    dve.tensor_scalar(r1[:, 0, t0:t1], mv1[:, t0:t1, 1], EPS, None,
                                      ALU.add).then_inc(var_ready, 1)
                elif name == "LNS":
                    t0, t1 = (0, NT) if b == 0 else (NT, NB * NT)
                    dve.wait_ge(std_ready, b + 1)
                    inverse_std(r1, t0, t1)
                elif name == "WT" and i == 3:
                    wait_filled(dve, "WT", 0, 3, 0)
                    dve.wait_ge(tanh_ready, 1)
                    drain(dve.tensor_scalar(WT[:, 3].rearrange("p c n -> p (c n)"),
                                            bank("WT", 0, 3, 0)[:, :], tg[:, 2:3], None, ALU.mult),
                          "WT", 0, 3, 0)
                elif name == "ROWS":
                    dve.wait_ge(loaded["rows"], 64)
                    link(dve.tensor_tensor(rows[:, 2, :], rows[:, 2, :], ob[:, 0, :], ALU.add))
                    link(dve.tensor_scalar(rows[:, 2, :], rows[:, 2, :], tg[:, 3:4], None, ALU.mult))
                    dve.tensor_scalar(rows[:, 1, :], rows[:, 1, :], tg[:, 2:3], None,
                                      ALU.mult).then_inc(tanh_ready, 1)
                elif name == "PAD":
                    dve.wait_ge(loaded["mask"], 32)
                    link(dve.tensor_copy(padf, pad_u8))
                    dve.tensor_scalar(padb, padf, NEG, None, ALU.mult).then_inc(pad_ready, 1)
                    link(dve.scalar_tensor_tensor(out=padt, in0=padf, scalar=1.0e6, in1=iota,
                                                  op0=ALU.mult, op1=ALU.add))
                    link(dve.tensor_reduce(first_key, padt, AX_X, ALU.min))
                    dve.tensor_scalar(allpad, iota, first_key, None,
                                      ALU.is_lt).then_inc(pad_ready, 1)
                elif name in ("XN", "LN2"):
                    k = xn_turn[("XT" if name == "XN" else "YT", b)]
                    if name == "LN2":
                        for t in range(NT):
                            wait_drained(dve, "OP", b, t, 0)
                            link(dve.bn_stats(lnst[:, t, :], X[:, NT * b + t, :]))
                            link(dve.bn_aggr(mv2[:, t, :], lnst[:, t, :]))
                        dve.tensor_scalar(r2[:, 0, :], mv2[:, :, 1], EPS, None,
                                          ALU.add).then_inc(var_ready, 1)
                        dve.wait_ge(std_ready, b + 3)
                        inverse_std(r2, 0, NT)
                    if k > 0:
                        prev = xn_keys[k - 1]
                        wait_filled(dve, *prev, 1)
                    mv, r, t0 = (mv1, r1, NT * b) if name == "XN" else (mv2, r2, 0)
                    for t in range(NT):
                        ins = dve.tensor_scalar(xn[:, t, :], X[:, NT * b + t, :],
                                                mv[:, t0 + t, 0:1], r[:, 2, t0 + t:t0 + t + 1],
                                                ALU.subtract, ALU.mult)
                    ins.then_inc(xn_ready, 1)
                elif name in ("QP", "KP"):
                    f, parts, split = (qf, qp, q_split) if name == "QP" else (kf, kp, k_split)
                    wait_drained(dve, name, b, i, 0)
                    link(dve.tensor_tensor(f[:, :], f[:, :], parts[:, 0, :], ALU.subtract))
                    link(dve.tensor_copy(parts[:, 1, :], f[:, :]))
                    dve.tensor_tensor(parts[:, 2, :], f[:, :], parts[:, 1, :],
                                      ALU.subtract).then_inc(split, 1)
                elif name == "VP":
                    if b >= 2:
                        dve.wait_ge(pv_done, 3 * HG * (b - 1))
                    if b == 1:
                        dve.wait_ge(value_const, 1)
                    if b == 0 and i == 0:
                        dve.wait_ge(const_ready, 1)
                    wait_filled(dve, "VP", b, i, 0)
                    pv = bank("VP", b, i, 0)[:, :].rearrange("p (u h d) -> p u h d", u=2, d=HD)
                    for u in range(2):
                        ins = dve.tensor_tensor(
                            Vs[b % 2][:, 2 * i + u, :, 0:HD], pv[:, u],
                            rows[:, 0, :].rearrange("p (h d) -> p h d", d=HD), ALU.add)
                    drain(ins, "VP", b, i, 0)
                elif name == "FT":
                    wait_filled(dve, "FT", 0, 0, 0)
                    drain(dve.tensor_copy(fcol, bank("FT", 0, 0, 0)[:, 0:NB * NT].rearrange(
                        "p (t b) -> p t b", b=NB)), "FT", 0, 0, 0)
                elif name == "CM":
                    dve.wait_ge(keys_summed, NB)
                    wait_filled(dve, "EW", 0, 3, 0)
                    dve.tensor_copy(csum, OACC[:, 0:D]).then_inc(csum_ready, 1)
                    wait_filled(dve, "CM", 0, 0, 0)
                    drain(dve.tensor_copy(cmT, bank("CM", 0, 0, 0)[:, 0:2 * P].rearrange(
                        "p (c b r) -> p c b r", c=KC, b=NB)[:, :, :, 0]), "CM", 0, 0, 0)
                elif name == "VM":
                    wait_filled(dve, "VM", 0, 0, 0)
                    dve.wait_ge(loaded["cols2"], 48)
                    for c in range(KC):
                        ins = dve.tensor_scalar(mvT[:, c, :], bank("VM", 0, 0, 0)[:, NB * c:NB * c + NB],
                                                bv_c[:, c:c + 1], None, ALU.add)
                    drain(ins, "VM", 0, 0, 0)
                elif name == "SM":
                    n = 10 * HG * b + i
                    if n == 0:
                        dve.wait_ge(tri_ready, 1)
                    if b > 0 and i % (5 * HG) == 0:
                        dve.wait_ge(negmax_ready, 2 * (b - 1) + i // (5 * HG) + 1)
                    dve.wait_ge(sm_filled, n + 1)
                    hp, u = divmod(i, 5)
                    h = 2 * hp + (u // 2 if u < 4 else 0)
                    blocks = (((h, 3, 0),) if u in (0, 2) else ((h, 0, 0), (h, 2, P))
                              if u in (1, 3) else ((h, 1, 0), (h + 1, 1, 2 * P)))
                    for hh, qt, at in blocks:
                        w = (qt + 1) * P
                        ins = dve.tensor_tensor_reduce(
                            out=SM[n % SM_RING][:, at:at + w], in0=SM[n % SM_RING][:, at:at + w],
                            in1=tri[:, T - w:T], scale=1.0, scalar=3.0 * NEG, op0=ALU.add,
                            op1=ALU.max, accum_out=rowmax[:, hh, qt:qt + 1])
                    ins.then_inc(max_done, 1)
                elif name == "MX":
                    dve.wait_ge(max_done, 10 * HG * b + 5 * HG * (i + 1))
                    m = rowmax[:, H // 2 * i:H // 2 * (i + 1), :].rearrange("p h t -> p (h t)")
                    neg = negmax[:, 2 * H * i:2 * H * (i + 1)]
                    dve.tensor_scalar(nokey[:, :], m, FLOOR, 2.0 * FLOOR, ALU.is_lt, ALU.mult)
                    link(dve.tensor_scalar(neg, m, FLOOR, -1.0, ALU.max, ALU.mult))
                    dve.tensor_tensor(neg, neg, nokey[:, :], ALU.add).then_inc(negmax_ready, 1)
                elif name == "MR":
                    if b > 0:
                        dve.wait_ge(maxrow_loaded[b - 1][i], 48)
                    wait_filled(dve, "MR", b, i, 0)
                    pm = bank("MR", b, i, 0)[0:2 * H, 0:P]
                    rest = mrest[:, :]
                    if 2 * b + i > 0:
                        dve.wait_ge(mparts_ready, 2 * b + i)
                    link(dve.tensor_copy(mparts[:, i, 0, :], pm))
                    drain(dve.tensor_tensor(rest, pm, mparts[:, i, 0, :], ALU.subtract),
                          "MR", b, i, 0)
                    wait_drained(dve, "MR", b, i, 0)
                    link(dve.tensor_copy(mparts[:, i, 1, :], rest))
                    dve.tensor_tensor(mparts[:, i, 2, :], rest, mparts[:, i, 1, :],
                                      ALU.subtract).then_inc(mparts_ready, 1)
                elif name == "NM":
                    wait_filled(dve, "NM", b, i, 0)
                    po = bank("NM", b, i, 0)[:, :].rearrange("p (t j c) -> p t j c", t=NT, c=32)
                    link(dve.tensor_scalar(den.rearrange("p (t j) -> p t j", j=4),
                                           po[:, :, :, HD], 1.0e-30, None, ALU.max))
                    link(dve.reciprocal(rden, den))
                    if b == 0 and i == 0:
                        wait_filled(dve, "WT", 0, 3, 0)
                    if b > 0 and i == 0:
                        wait_filled(dve, "OT", b - 1, 0, 1)
                    drain(dve.tensor_tensor(
                        On_v[:, :, 64 * i:64 * i + 64].rearrange("p t (j d) -> p t j d", d=HD),
                        po[:, :, :, 0:HD],
                        rden.rearrange("p (t j) -> p t j", j=4).unsqueeze(3).to_broadcast(
                            [P, NT, 4, HD]), ALU.mult), "NM", b, i, 0)
                elif name == "OP":
                    wait_filled(dve, "OP", b, i, 0)
                    dve.wait_ge(base_ready, NT * b + i + 1)
                    xt = X[:, NT * b + i, :]
                    drain(dve.tensor_tensor(xt, bank("OP", b, i, 0)[:, 0:D], xt, ALU.add),
                          "OP", b, i, 0)
                elif name == "F2":
                    wait_filled(dve, "F2", b, i, 0)
                    dve.wait_ge(y_based, NT * b + i + 1)
                    if NT * b + i >= 2:
                        dve.wait_ge(stored[i % 2], 16 * ((NT * b + i) // 2))
                    ins = dve.tensor_tensor(ob[:, i % 2, :], bank("F2", b, i, 0)[:, 0:D],
                                            X[:, NT * b + i, :], ALU.add)
                    drain(ins, "F2", b, i, 0)
                elif name == "EW" and i == 3:
                    wait_drained(dve, "EW", 0, 3, 0)
                    dve.wait_ge(loaded["cols2"], 48)
                    dve.tensor_copy(upY[:, :, D], bexp_c).then_inc(wexpT_ready, 1)
                elif name == "SEL":
                    wait_filled(dve, "SEL", b, i, 0)
                    n = 1 << b
                    src = chain_odd if b % 2 else chain_even
                    dst = chain_even if b % 2 else chain_odd
                    pw = bank("SEL", b, i, 0)
                    if b < 5:
                        parts = [(w, 0, NI, 16 * n * w) for w in range(2)]
                    elif b == 5:
                        parts = [(i, 0, NI, 0)]
                    else:
                        parts = [(i // 2, 4 * (i % 2), 4, 0)]
                    for w, t0, nt, at in parts:
                        d = dst[:, w, 0:2 * NI * n].rearrange("p (t a u) -> p t a u", a=2, u=n)[
                            :, t0:t0 + nt]
                        f = pw[:, at:at + 2 * nt * n].rearrange("p (t a u) -> p t a u", a=2, u=n)
                        if b == 0:
                            ins = dve.tensor_copy(d, f)
                        else:
                            s = src[:, w, 0:NI * n].rearrange("p (t u) -> p t u", u=n)[
                                :, t0:t0 + nt].unsqueeze(2).to_broadcast([P, nt, 2, n])
                            ins = dve.tensor_tensor(d, f, s, ALU.mult)
                    drain(ins, "SEL", b, i, 0)
                    wait_drained(dve, "SEL", b, i, 0)
                elif name == "UST":
                    if i == 0:
                        dve.wait_ge(loaded["stage79"], 16 * 2 * (STAGES - LOW))
                        wait_drained(dve, "UB", 0, NI - 1, 0)
                    ta, tb = up_tmp
                    a, c, w = list(pairs(i // PAIRS, 0))[i % PAIRS]
                    dve.tensor_scalar(ta, upY[:, a, :], w[:, 0:1], None, ALU.mult)
                    link(dve.tensor_scalar(tb, upY[:, a, :], w[:, 2:3], None, ALU.mult))
                    dve.scalar_tensor_tensor(out=upY[:, a, :], in0=upY[:, c, :],
                                             scalar=w[:, 1:2], in1=ta, op0=ALU.mult, op1=ALU.add)
                    link(dve.scalar_tensor_tensor(out=upY[:, c, :], in0=upY[:, c, :],
                                                  scalar=w[:, 3:4], in1=tb,
                                                  op0=ALU.mult, op1=ALU.add))
                    if i == (STAGES - LOW) * PAIRS - 1:
                        dve.tensor_tensor(hb, upY[:, :, D], upb_c, ALU.add).then_inc(up_staged, 1)
                elif name == "DST":
                    if i == 0:
                        dve.wait_ge(down_top_staged, 1)
                    ta, tb = down_tmp
                    a, c, w = list(pairs(1 - i // PAIRS, 1))[i % PAIRS]
                    dve.tensor_scalar(ta, Wd[:, a, :], w[:, 0:1], None, ALU.mult)
                    link(dve.tensor_scalar(tb, Wd[:, a, :], w[:, 1:2], None, ALU.mult))
                    dve.scalar_tensor_tensor(out=Wd[:, a, :], in0=Wd[:, c, :],
                                             scalar=w[:, 2:3], in1=ta, op0=ALU.mult, op1=ALU.add)
                    ins = dve.scalar_tensor_tensor(out=Wd[:, c, :], in0=Wd[:, c, :],
                                                   scalar=w[:, 3:4], in1=tb,
                                                   op0=ALU.mult, op1=ALU.add)
                    if i < 2 * PAIRS - 1:
                        link(ins)
                    else:
                        ins.then_inc(down_staged, 1)

        @block.tensor
        def _(pe):
            def take(*key):
                n = turn[key]
                if n >= MISC:
                    pe.wait_ge(drained[n % MISC], n // MISC)
                return MB[n % MISC]

            def fill(ins, *key):
                ins.then_inc(filled[turn[key] % MISC], 1)

            def transposes(blocks, *key):
                dst = take(*key)
                for n, src in enumerate(blocks):
                    ins = pe.transpose(dst[:, P * n:P * n + P], src, ident[:, :])
                fill(ins, *key)

            pe.wait_ge(loaded["ident"], 16)
            for name, b, i in order:
                if name == "WT":
                    pe.wait_ge(loaded[f"w{i}"], 16)
                    transposes([wraw[:, i, m, P * c:P * c + P] for c in range(KC)
                                for m in range(KC)], "WT", 0, i, 0)
                elif name in ("XT", "YT"):
                    pe.wait_ge(xn_ready, xn_turn[(name, b)] + 1)
                    for c in range(KC):
                        transposes([xn[:, t, P * c:P * c + P] for t in range(NT)], name, b, i, c)
                elif name == "CT":
                    pe.wait_ge(ctx_loaded[b], 16)
                    for c in range(KC):
                        transposes([ctxA[:, t, P * c:P * c + P] for t in range(NT)], name, b, i, c)
                elif name in ("QP", "KP"):
                    w, src, key = (0, xnT, "XT") if name == "QP" else (1, ctxT, "CT")
                    if b == 0:
                        wait_drained(pe, "WT", 0, w, 0)
                    wait_drained(pe, key, b, 0, KC - 1)
                    dst = take(name, b, i, 0)
                    for c in range(KC):
                        ins = pe.matmul(dst[:, :], WT[:, w, c, P * i:P * i + P], src[:, c, :],
                                        start=(c == 0), stop=(c == KC - 1))
                    fill(ins, name, b, i, 0)
                elif name == "VP":
                    dst = take(name, b, i, 0)
                    if b == 0:
                        wait_drained(pe, "WT", 0, 2, 0)
                    for u in range(2):
                        kt = 2 * i + u
                        for c in range(KC):
                            ins = pe.matmul(dst[:, D * u:D * u + D], ctxT[:, c, P * kt:P * kt + P],
                                            WT[:, 2, c, :], start=(c == 0), stop=(c == KC - 1))
                    fill(ins, name, b, i, 0)
                elif name == "FT":
                    pe.wait_ge(pad_ready, 2)
                    dst = take(name, b, i, 0)
                    for t in range(NT):
                        ins = pe.transpose(dst[:, NB * t:NB * t + NB], allpad[:, P * t:P * t + P],
                                           ident[0:NB, 0:NB])
                    fill(ins, name, b, i, 0)
                elif name == "CS":
                    if i == 0:
                        pe.wait_ge(const_ready, 1)
                    pe.wait_ge(keys_added, i + 1)
                    pe.matmul(OACC[32 * i:32 * i + 32, 0:D], mean32[:, :], keys_sum[:, i, :],
                              start=True, stop=True).then_inc(keys_summed, 1)
                elif name == "CM":
                    pe.wait_ge(csum_ready, 1)
                    transposes([csum[:, P * c:P * c + P] for c in range(KC)], name, b, i, 0)
                elif name == "VM":
                    wait_drained(pe, "CM", 0, 0, 0)
                    dst = take(name, b, i, 0)
                    for m in range(KC):
                        for c in range(KC):
                            ins = pe.matmul(dst[:, NB * m:NB * m + NB],
                                            WT[:, 2, c, P * m:P * m + P], cmT[:, c, :],
                                            start=(c == 0), stop=(c == KC - 1))
                    fill(ins, name, b, i, 0)
                elif name == "MP":
                    wait_drained(pe, "VM", 0, 0, 0)
                    dst = take(name, b, i, 0)
                    for c in range(KC):
                        ins = pe.matmul(dst[:, 0:D], mvT[:, c, i:i + 1].to_broadcast([P, P]),
                                        WT[:, 3, c, :], start=(c == 0), stop=(c == KC - 1))
                    fill(ins, name, b, i, 0)
                elif name == "EW":
                    if i == 0:
                        pe.wait_ge(loaded["wexp"], 16)
                    transposes([wexp[:, c, P * t:P * t + P] for t in (2 * i, 2 * i + 1)
                                for c in range(KC)], name, b, i, 0)
                elif name == "SEL":
                    if b == 0:
                        pe.wait_ge(loaded["select"], 16)
                        pe.wait_ge(loaded["wlow"], 16 * 2 * LOW)
                    dst = take(name, b, i, 0)
                    n = 1 << b
                    if b < 5:
                        parts = [(wlow_of(b)[:, w], 16 * n * w) for w in range(2)]
                    elif b == 5:
                        parts = [(wlow_of(b)[:, i], 0)]
                    else:
                        parts = [(wlow6[:, i // 2, 4 * (i % 2):4 * (i % 2) + 4, :], 0)]
                    for src, at in parts:
                        v = src.rearrange("q t (u a c) -> q t a u c", a=2, c=2)
                        nt = v.shape[1]
                        for bit in range(2):
                            ins = pe.matmul(dst[:, at:at + 2 * nt * n],
                                            esel[64 * (b == 6):64 * (b == 6) + (64 >> b),
                                                 2 * b + bit, :], v[:, :, :, :, bit],
                                            start=(bit == 0), stop=(bit == 1))
                    fill(ins, name, b, i, 0)
                elif name == "DTR":
                    wait_drained(pe, "SEL", LOW - 1, 3, 0)
                    transposes([chain_odd[:, 1, P * t:P * t + P] for t in range(4 * i, 4 * i + 4)],
                               name, b, i, 0)
                elif name == "UB":
                    wait_drained(pe, "EW", 0, 3, 0)
                    if i == 0:
                        pe.wait_ge(wexpT_ready, 1)
                    dst = take(name, b, i, 0)
                    fill(pe.matmul(dst[:, 0:D + 1], chain_odd[:, 0, P * i:P * i + P],
                                   upY[:, i, :], start=True, stop=True), name, b, i, 0)
                elif name == "DB":
                    pe.wait_ge(down_staged, 1)
                    wait_drained(pe, "DTR", 0, 1, 0)
                    dst = take(name, b, i, 0)
                    for u in range(2):
                        ins = pe.matmul(dst[:, D * u:D * u + D], dnT[:, 2 * i + u, :],
                                        Wd[:, 2 * i + u, :], start=True, stop=True)
                    fill(ins, name, b, i, 0)
                elif name == "UT":
                    pe.wait_ge(up_staged, 1)
                    c, half = divmod(i, 2)
                    transposes([upY[:, 4 * half + t, P * c:P * c + P] for t in range(4)],
                               name, b, i, 0)
                elif name == "SM":
                    n = 10 * HG * b + i
                    if i % (5 * HG) == 0:
                        pe.wait_ge(stack_loaded[b][i // (5 * HG)],
                                   16 * (2 * len(TERM_RUNS) + (i == 0)))
                        if b < 2 and i == 0:
                            pe.wait_ge(loaded[f"ones{b}"], 32)
                    if n >= SM_RING:
                        pe.wait_ge(max_done, n - SM_RING + 1)
                    hp, u = divmod(i, 5)
                    h = 2 * hp + (u // 2 if u < 4 else 0)
                    blocks = (((h, 3, 0),) if u in (0, 2) else ((h, 0, 0), (h, 2, P))
                              if u in (1, 3) else ((h, 1, 0), (h + 1, 1, 2 * P)))
                    for hh, qt, at in blocks:
                        w = (qt + 1) * P
                        ins = pe.matmul(SM[n % SM_RING][:, at:at + w],
                                        Qs[b % 2][0:KROWS + 1, hh, P * qt:P * qt + P],
                                        Ks[b % 2][0:KROWS + 1, hh, 0:w], start=True, stop=True)
                    ins.then_inc(sm_filled, 1)
                elif name == "MR":
                    pe.wait_ge(negmax_ready, 2 * b + i + 1)
                    dst = take(name, b, i, 0)
                    fill(pe.transpose(dst[0:2 * H, 0:P], negmax[:, 2 * H * i:2 * H * (i + 1)],
                                      ident[:, :]), name, b, i, 0)
                elif name == "ST":
                    n = 10 * HG * b + i
                    if i % (5 * HG) == 0:
                        pe.wait_ge(maxrow_loaded[b][i // (5 * HG)], 48)
                    if n >= ST_RING:
                        pe.wait_ge(exp_done, n - ST_RING + 1)
                    g, r = divmod(i, 10)
                    blocks = (((4 * g + r, 0, 0),) if r < 4 else
                              ((4 * g + r - 4, 1, 0), (4 * g + r - 4, 3, 3 * P)) if r < 8 else
                              ((4 * g + 2 * (r - 8), 2, 0), (4 * g + 2 * (r - 8) + 1, 2, 2 * P)))
                    for h, kt, at in blocks:
                        w = T - P * kt
                        ins = pe.matmul(ST[n % ST_RING][:, at:at + w],
                                        Ks[b % 2][0:KROWS + 4, h, P * kt:P * kt + P],
                                        Qs[b % 2][0:KROWS + 4, h, P * kt:T], start=True, stop=True)
                    ins.then_inc(st_filled, 1)
                elif name == "PV":
                    g, part = divmod(i, 3)
                    G = HG * b + g
                    n0 = 10 * G
                    if i == 0:
                        wait_drained(pe, "VP", b, 1, 0)
                    if part == 0:
                        pe.wait_ge(oacc_drained, G) if G else pe.wait_ge(csum_ready, 1)
                    pe.wait_ge(mask_done, n0 + (4, 8, 10)[part])
                    for kt in ((0,), (1, 3), (2,))[part]:
                        for j in range(4):
                            n = n0 + (j if part == 0 else 4 + j if part == 1 else 8 + j // 2)
                            at = T * (n % P_RING) + (3 * P if kt == 3 else
                                                     2 * P * (j % 2) if kt == 2 else 0)
                            ins = pe.matmul(OACC[32 * j:32 * j + 32, P * kt:T],
                                            Vs[b % 2][:, kt, 4 * g + j, :],
                                            probs[:, at:at + T - P * kt],
                                            start=(kt == 0), stop=(kt == 2))
                    ins.then_inc(pv_done, 1)
                elif name == "NM":
                    pe.wait_ge(oacc_drained, HG * b + i + 1)
                    transposes([oT[:, (HG * b + i) % 2, P * t:P * t + P] for t in range(NT)],
                               name, b, i, 0)
                elif name == "OT":
                    wait_drained(pe, "NM", b, HG - 1, 0)
                    for c in range(KC):
                        transposes([On_v[:, t, P * c:P * c + P] for t in range(NT)], name, b, i, c)
                elif name == "OP":
                    wait_drained(pe, "OT", b, 0, KC - 1)
                    dst = take(name, b, i, 0)
                    for c in range(KC):
                        ins = pe.matmul(dst[:, 0:D], OnT[:, c, P * i:P * i + P], WT[:, 3, c, :],
                                        start=(c == 0), stop=(c == KC - 1))
                    fill(ins, name, b, i, 0)
                elif name == "F1":
                    wait_drained(pe, "YT", b, 0, KC - 1)
                    if b == 0 and i == 0:
                        wait_drained(pe, "UT", 0, 3, 0)
                    dst = take(name, b, i, 0)
                    for c in range(KC):
                        ins = pe.matmul(dst[:, :], Wu[:, c, P * i:P * i + P], xnT[:, c, :],
                                        start=(c == 0), stop=(c == KC - 1))
                    fill(ins, name, b, i, 0)
                elif name == "F2":
                    wait_drained(pe, "F1", b, NI - 1, 0)
                    if b == 0 and i == 0:
                        wait_drained(pe, "DB", 0, 3, 0)
                    dst = take(name, b, i, 0)
                    for n in range(NI):
                        ins = pe.matmul(dst[:, 0:D], hT[:, n, P * i:P * i + P], Wd[:, n, :],
                                        start=(n == 0), stop=(n == NI - 1))
                    fill(ins, name, b, i, 0)


_INS = ["x", "ctx_1024", "mask_BxS2_bf0", "g_xattn", "g_ffn", "L0_xattn_Wq", "L0_xattn_bq",
        "L0_xattn_Wk", "L0_xattn_bk", "L0_xattn_Wv", "L0_xattn_bv", "L0_xattn_Wo", "L0_xattn_bo",
        "L0_ffn_W_exp", "L0_ffn_b_exp", "L0_ffn_up_weights", "L0_ffn_up_bias",
        "L0_ffn_down_weights", "L0_ffn_W_con", "L0_ffn_b_con", "L0_ffn_down_bias"]


def _constants(NB, T):
    import numpy as np

    j = np.arange(P)
    select = np.zeros((65, 2 * 7, P), np.float32)
    for k in range(7):
        for bit in range(2):
            r = 64 * (k == 6)
            select[r:r + (64 >> k), 2 * k + bit] = (j >> k)[None, :] == 2 * np.arange(64 >> k)[:, None] + bit
    return {"ident": np.eye(P, dtype=np.float32),
            "iota": np.tile(np.arange(T, dtype=np.float32), (NB, 1)), "select": select}


def kernel(**inputs):
    import numpy as _np
    import concourse.bacc as _bacc
    from concourse import mybir as _mybir
    from concourse.bass_utils import run_bass_kernel_spmd as _run

    nc = _bacc.Bacc("TRN2", target_bir_lowering=False, num_devices=1)
    arrays, args = {}, []
    given = [(n, _np.ascontiguousarray(inputs[n])) for n in _INS]
    NB, T, D = given[0][1].shape
    given += list(_constants(NB, T).items())
    for name, a in given:
        arrays[f"in_{name}_dram"] = a
        args.append(nc.dram_tensor(f"in_{name}_dram", a.shape, _mybir.dt.from_np(a.dtype),
                                   kind="ExternalInput").ap())
    args.append(nc.dram_tensor("out_0_dram", (NB, T, D), _mybir.dt.float32,
                               kind="ExternalOutput").ap())
    flamingo_block(nc, *args)
    r = _run(nc, [arrays], core_ids=[0])
    return r.results[0]["out_0_dram"]
```
